# Optimizing a Trainium2 kernel written in Bass

```python
import numpy as np
import jax
import jax.numpy as jnp

def _softmax(x, axis=-1):
    return jax.nn.softmax(x, axis=axis)

def _gelu(x):
    return jax.nn.gelu(x, approximate=True)

def _silu(x):
    return jax.nn.silu(x)

def _sigmoid(x):
    return jax.nn.sigmoid(x)

def _layernorm(x, axis=-1, eps=1e-05):
    m = jnp.mean(x, axis=axis, keepdims=True)
    v = jnp.var(x, axis=axis, keepdims=True)
    return (x - m) / jnp.sqrt(v + eps)

def _scatter_add(tgt, idx, src, axis=0):
    return tgt.at[idx].add(src)

def _segment_sum(src, seg, n):
    return jax.ops.segment_sum(src, seg, n)
kernel_name = 'mk_adaln_d1_jaxref_r8_0d29f3'

def setup_inputs(seed: int=0):
    np.random.seed(seed)
    _w = jnp.asarray

    def _L0_attn_setup():
        import jax, jax.numpy as jnp
        import numpy as np
        EPS = 1.1920929e-07

        def _rms(x):
            return x * jax.lax.rsqrt(jnp.mean(x * x, axis=-1, keepdims=True) + EPS)
        key = jax.random.key(seed)
        k0, k1, k2, k3 = jax.random.split(key, 4)
        B, S, D, DFF = (4, 256, 256, 1024)
        x = jax.random.normal(k0, (B, S, D), dtype=jnp.float32)
        w_qkv = jax.random.normal(k1, (3 * D, D), dtype=jnp.float32) * 0.02
        w_swiglu = jax.random.normal(k2, (2 * DFF, D), dtype=jnp.float32) * 0.02
        w_out = jax.random.normal(k3, (D, DFF), dtype=jnp.float32) * 0.02
        return {'x': x, 'w_qkv': w_qkv, 'w_swiglu': w_swiglu, 'w_out': w_out}
    _L0_attn_in = _L0_attn_setup()

    def _L0_ffn_setup():
        import jax, jax.numpy as jnp
        import numpy as np
        DIM_IN = 256
        DIM_HIDDEN = 1024
        key = jax.random.key(seed)
        k_x, k_g, k_u, k_d = jax.random.split(key, 4)
        s_in = 1.0 / np.sqrt(DIM_IN)
        s_hid = 1.0 / np.sqrt(DIM_HIDDEN)
        x = jax.random.normal(k_x, (4, 256, DIM_IN), dtype=jnp.float32)
        w_gate = jax.random.uniform(k_g, (DIM_HIDDEN, DIM_IN), jnp.float32, -s_in, s_in)
        w_up = jax.random.uniform(k_u, (DIM_HIDDEN, DIM_IN), jnp.float32, -s_in, s_in)
        w_down = jax.random.uniform(k_d, (DIM_IN, DIM_HIDDEN), jnp.float32, -s_hid, s_hid)
        return {'x': x, 'w_gate': w_gate, 'w_up': w_up, 'w_down': w_down}
    _L0_ffn_in = _L0_ffn_setup()
    _L0_c = _w((lambda *s: np.random.randn(*s).astype(np.float32) * 0.05)(1, 256))
    _L0_wmod = _w((lambda *s: np.random.randn(*s).astype(np.float32) * 0.05)(256, 6 * 256) * 256 ** (-0.5))
    _d = {'L0_attn_x': _L0_attn_in['x'], 'L0_attn_w_qkv': _L0_attn_in['w_qkv'], 'L0_attn_w_swiglu': _L0_attn_in['w_swiglu'], 'L0_attn_w_out': _L0_attn_in['w_out'], 'L0_ffn_w_gate': _L0_ffn_in['w_gate'], 'L0_ffn_w_up': _L0_ffn_in['w_up'], 'L0_ffn_w_down': _L0_ffn_in['w_down'], 'L0_c': _L0_c, 'L0_wmod': _L0_wmod}
    _x0 = _d['L0_attn_x']
    _d['L0_attn_x'] = jax.random.normal(jax.random.fold_in(jax.random.key(seed), 1), (1, 2048, 256), dtype=_x0.dtype)
    del _x0
    return _d

def reference(L0_attn_x, L0_attn_w_qkv, L0_attn_w_swiglu, L0_attn_w_out, L0_ffn_w_gate, L0_ffn_w_up, L0_ffn_w_down, L0_c, L0_wmod):

    def _L0_attn_ref(x, w_qkv, w_swiglu, w_out):
        import jax, jax.numpy as jnp
        import numpy as np
        EPS = 1.1920929e-07

        def _rms(x):
            return x * jax.lax.rsqrt(jnp.mean(x * x, axis=-1, keepdims=True) + EPS)
        qkv = _rms(x) @ w_qkv.T
        q, k, v = jnp.split(qkv, 3, axis=-1)
        q = _rms(q)
        k = _rms(k)
        w = jnp.exp(k)
        kv_cum = jnp.cumsum(w * v, axis=1)
        w_cum = jnp.cumsum(w, axis=1)
        y = jax.nn.sigmoid(q) * (kv_cum / (w_cum + 1e-06))
        uv = y @ w_swiglu.T
        u, g = jnp.split(uv, 2, axis=-1)
        return x + u * jax.nn.silu(g) @ w_out.T

    def _L0_ffn_ref(x, w_gate, w_up, w_down):
        import jax, jax.numpy as jnp
        import numpy as np
        DIM_IN = 256
        DIM_HIDDEN = 1024
        gate = jnp.einsum('bsd,hd->bsh', x, w_gate)
        up = jnp.einsum('bsd,hd->bsh', x, w_up)
        gated = jax.nn.silu(gate) * up
        return jnp.einsum('bsh,dh->bsd', gated, w_down)
    x = L0_attn_x
    mod = (_silu(L0_c) @ L0_wmod).reshape(L0_c.shape[0], 6, 1, -1)
    sa, ca, ga, sb, cb, gb = (mod[:, 0], mod[:, 1], mod[:, 2], mod[:, 3], mod[:, 4], mod[:, 5])
    ga = (2 * (ga >= 0) - 1) * jnp.maximum(jnp.abs(ga), 0.25)
    gb = (2 * (gb >= 0) - 1) * jnp.maximum(jnp.abs(gb), 0.25)
    h = _layernorm(x, axis=-1) * (1 + ca) + sa
    x = x + ga * _L0_attn_ref(h, L0_attn_w_qkv, L0_attn_w_swiglu, L0_attn_w_out)
    h = _layernorm(x, axis=-1) * (1 + cb) + sb
    x = x + gb * _L0_ffn_ref(h, L0_ffn_w_gate, L0_ffn_w_up, L0_ffn_w_down)
    return x

_drawn_inputs = setup_inputs


def setup_inputs(seed=0):
    import zlib

    import numpy as np

    out = dict(_drawn_inputs(seed))
    spreads = {}
    factors = {'L0_attn_w_qkv': 8.0,
     'L0_attn_w_swiglu': 8.0,
     'L0_attn_w_out': 8.0,
     'L0_ffn_w_gate': 8.0,
     'L0_ffn_w_up': 8.0,
     'L0_ffn_w_down': 8.0}
    for name, (base, spread) in spreads.items():
        noise = np.random.default_rng([zlib.crc32(name.encode()), seed]).standard_normal(out[name].shape)
        drawn = base * np.exp(spread * noise) if base else spread * noise
        out[name] = jnp.asarray(drawn.astype(out[name].dtype))
    for name, factor in factors.items():
        out[name] = (out[name] * factor).astype(out[name].dtype)
    return out
```

```python
import concourse.bass as bass
from concourse import mybir
from contextlib import ExitStack

P = 128
S, D, F = 2048, 256, 1024
CH = 512
NC = S // CH
TT = CH // P
KD = D // P
J = F // P
LN_EPS = 1e-05
RMS_EPS = 1.1920929e-07
CUM_EPS = 1e-06
GATE_MIN = 0.25

MIX, FFN = 0, 1
BLOCKS = [(MIX, 0)]
for _c in range(NC - 1):
    BLOCKS += [(MIX, _c + 1), (FFN, _c)]
BLOCKS.append((FFN, NC - 1))
NB = len(BLOCKS)
LN_EXP, SILU = "natural_log_exp_and_others", "silu_and_others"
LAG = 2
HS_SLOTS = LAG + 1

PROJECT_IN = {1: 2, 3: 3}
SCAN_IN = {0: 1, 2: 2, 4: 3}
SCAN_AT = {0: 2, 2: 1, 4: 1}

TRANSIT = [(w, 0) for w in "hkqvs"] + [(w, 1) for w in "hkqvs"]
for _b in range(1, NB + 1):
    _mix = BLOCKS[_b - 1][0] == MIX
    if _b in PROJECT_IN:
        TRANSIT += [("back", _b - 1)] + [(w, PROJECT_IN[_b]) for w in "hkq"]
        TRANSIT += [("x", BLOCKS[_b - 1][1])] * _mix + [("v", PROJECT_IN[_b])]
    else:
        TRANSIT += [("s", SCAN_IN.get(_b))] * (_b in SCAN_IN) + [("back", _b - 1)]
        TRANSIT += [("x", BLOCKS[_b - 1][1])] * _mix


PARTS = "kqv"


def turn(what, which):
    return TRANSIT.index((what, which))


def adaln_kernel(nc, x_d, c_d, wmod_d, wqkv_d, wmix_up_d, wmix_out_d, wffn_up_d, wffn_down_d, out_d):
    f32, f32r = mybir.dt.float32, mybir.dt.float32r
    ACT, ALU = mybir.ActivationFunctionType, mybir.AluOpType
    ctx = ExitStack()
    with ctx:
        at = [(nc.sbuf_base + 63) // 64 * 64]
        names = {}

        def place(name, shape, dt, offset=None):
            size = 4
            for n in shape[1:]:
                size *= n
            if offset is None:
                offset = at[0]
                at[0] += (size + 31) // 32 * 32
                assert at[0] <= nc.sbuf_usable_end, (name, at[0])
            names[name] = offset
            return nc.alloc_sbuf_tensor_at(name, shape, dt, offset=offset)

        def split_pair(name, shape):
            hi = place(name + "_hi", shape, f32r)
            lo = place(name + "_lo", shape, f32r)
            return hi, lo, place(name + "_raw", shape, f32, offset=names[name + "_lo"])

        wqkv_hi, wqkv_lo, wqkv_raw = split_pair("wqkv", [P, 3, KD, D])
        up_hi, up_lo, up_raw, down_hi, down_lo, down_raw = ([None, None] for _ in range(6))
        for layer, name in ((MIX, "mix"), (FFN, "ffn")):
            up_hi[layer], up_lo[layer], up_raw[layer] = split_pair(name + "_up", [P, J, KD, 2, P])
            down_hi[layer], down_lo[layer], down_raw[layer] = split_pair(name + "_down", [P, J, D])

        tok = place("tok", [P, NC, TT, D], f32)
        h_tok = place("h_tok", [P, TT, D], f32)
        hs_tok = place("hs_tok", [P, TT, D], f32)
        x2_tok = place("x2_tok", [P, TT, D], f32)
        out_fm = place("out_fm", [P, KD, CH], f32)
        x2_fm = place("x2_fm", [P, KD, CH], f32, offset=names["out_fm"])
        h_hi, h_lo = (place(n, [P, KD, CH], f32r) for n in ("h_hi", "h_lo"))
        y_hi, y_lo = (place(n, [P, KD, CH], f32r) for n in ("y_hi", "y_lo"))
        x2_hi, x2_lo = (place(n, [P, KD, CH], f32r) for n in ("x2_hi", "x2_lo"))
        q_fm, k_fm, v_fm = (place(n, [P, KD, CH], f32) for n in ("q_fm", "k_fm", "v_fm"))
        sq_q = place("sq_q", [P, KD, CH], f32, offset=names["hs_tok"])
        sq_k = place("sq_k", [P, KD, CH], f32, offset=names["h_tok"])
        sq_k0 = place("sq_k0", [P, KD, CH], f32, offset=names["x2_tok"])
        ss_hi, ss_lo = (place(n, [P, 2, CH], f32r) for n in ("ss_hi", "ss_lo"))
        hid = place("hid", [P, 2, CH], f32)
        hid_hi = place("hid_hi", [P, HS_SLOTS, CH], f32r)
        hid_lo = place("hid_lo", [P, HS_SLOTS, CH], f32r)
        wmod = place("wmod", [P, KD, 6 * D], f32, offset=names["hid_hi"])
        assert names["hid_lo"] == names["hid_hi"] + HS_SLOTS * CH * 4 and KD * 6 * D == 2 * HS_SLOTS * CH
        mod_scale, mod_shift, gate_tok = (place(n, [P, D], f32) for n in ("mod_scale", "mod_shift", "gate_tok"))
        ident = place("ident", [P, P], f32)
        ones_r = place("ones_r", [P, P], f32r)
        ones = place("ones", [P, P], f32, offset=names["x2_hi"])
        silu_c = place("silu_c", [P, KD], f32)
        silu_c_wide = place("silu_c_wide", [P, KD, P], f32, offset=names["x2_lo"])
        c_sb = place("c_sb", [P, KD], f32)
        cols = place("cols", [P, 6, KD], f32)
        col_t = place("col_t", [P, 2, KD], f32)
        stats = place("stats", [P, TT, 6], f32)
        mean_var = place("mean_var", [P, TT, 2], f32)
        rstd = place("rstd", [P, TT], f32)
        stats2 = place("stats2", [P, TT, 6], f32)
        mean_var2 = place("mean_var2", [P, TT, 2], f32)
        rstd2 = place("rstd2", [P, TT], f32)
        h_sum = place("h_sum", [P, TT], f32)
        h_rms = place("h_rms", [P, TT], f32)
        minus_half = place("minus_half", [P, TT], f32)
        one_col = place("one_col", [P, 1], f32)
        eps_col = place("eps_col", [P, 1], f32)
        carry = place("carry", [P, 2, KD], f32)

        def pb(name):
            return ctx.enter_context(nc.psum_tensor(name, [P, CH], f32))

        gate_ps = [pb(f"gate_ps{n}") for n in range(2)]
        up_ps = [pb(f"up_ps{n}") for n in range(2)]
        out_ps = [pb(f"out_ps{n}") for n in range(KD)]
        tr_ps = [pb(f"tr_ps{n}") for n in range(2)]
        r_q = sq_q[:, 0, :]

        def k_squares(c):
            return sq_k0 if c == 0 else sq_k

        def sem(name):
            return ctx.enter_context(nc.semaphore(name))

        c_in, wqkv_in = sem("c_in"), sem("wqkv_in")
        wmod_in = [sem(f"wmod_in{n}") for n in range(2)]
        tok_in = [sem(f"tok_in{n}") for n in range(NC)]
        up_in, down_in = ([sem(f"{n}_in{layer}") for layer in (MIX, FFN)] for n in ("up", "down"))
        consts, ident_ok, ones_ok = sem("consts"), sem("ident_ok"), sem("ones_ok")
        silu_c_ok, wide_ok = sem("silu_c_ok"), sem("wide_ok")
        mod_ps_ok, mod_ok, cols_ok = sem("mod_ps_ok"), sem("mod_ok"), sem("cols_ok")
        dve_step, pool_step, act_step = sem("dve_step"), sem("pool_step"), sem("act_step")
        wqkv_hi_ok, wqkv_lo_ok = sem("wqkv_hi_ok"), sem("wqkv_lo_ok")
        w_hi_ok = [sem(f"w_hi_ok{layer}") for layer in (MIX, FFN)]
        w_lo_ok = [[sem(f"w_lo_ok{layer}_{j}") for j in range(J)] for layer in (MIX, FFN)]
        stats_ok, rstd_ok, norm_ok = sem("stats_ok"), sem("rstd_ok"), sem("norm_ok")
        h_ok, h_sum_ok, h_rms_ok, hs_ok = sem("h_ok"), sem("h_sum_ok"), sem("h_rms_ok"), sem("hs_ok")
        resid_ok = sem("resid_ok")
        tr_full = [sem(f"tr_full{n}") for n in range(2)]
        tr_free = [sem(f"tr_free{n}") for n in range(2)]
        h_hi_ok, h_lo_ok = sem("h_hi_ok"), sem("h_lo_ok")
        sq_ok, ss_ok, qkv_ok = sem("sq_ok"), sem("ss_ok"), sem("qkv_ok")
        rk_ok, rq_ok, kn_ok, qn_ok, w_ok, e_ok = (sem(n) for n in ("rk_ok", "rq_ok", "kn_ok", "qn_ok", "w_ok", "e_ok"))
        den_ok, ln_ok, guess_ok = sem("den_ok"), sem("ln_ok"), sem("guess_ok")
        y_ok, y_hi_ok, y_lo_ok = (sem(n) for n in ("y_ok", "y_hi_ok", "y_lo_ok"))
        gate_full, up_full, silu_ok, hid_ok, hid_hi_ok, hid_lo_ok, down_done = (
            sem(n) for n in ("gate_full", "up_full", "silu_ok", "hid_ok", "hid_hi_ok", "hid_lo_ok", "down_done"))
        out_taken, x2_ok, stats2_ok, rstd2_ok = sem("out_taken"), sem("x2_ok"), sem("stats2_ok"), sem("rstd2_ok")
        x2_fm_ok, x2_hi_ok, x2_lo_ok = sem("x2_fm_ok"), sem("x2_hi_ok"), sem("x2_lo_ok")
        final_ok, stored = sem("final_ok"), sem("stored")


        def sums_of_squares(engine, wait_ge, link, c):
            for n, (what, sq) in enumerate((("k", k_squares(c)), ("q", sq_q))):
                for f in range(KD):
                    wait_ge(tr_free[f], turn(what, c) + 1)
                if c >= 1:
                    wait_ge(tr_full[n], turn("s", c - 1) + 1)
                link(engine.tensor_tensor(sq[:, 0, :], sq[:, 0, :], sq[:, 1, :], ALU.add))
                link(engine.tensor_scalar(ss_hi[:, n, :], sq[:, 0, :], 1.0, 0.0, ALU.mult, ALU.add))
                engine.tensor_tensor(ss_lo[:, n, :], sq[:, 0, :], ss_hi[:, n, :].bitcast(f32), ALU.subtract).then_inc(ss_ok, 1)

        def split_lo(engine, wait_ge, layer, j):
            wait_ge(w_hi_ok[layer], 2 * j + 2)
            for hi, lo, raw in ((up_hi, up_lo, up_raw), (down_hi, down_lo, down_raw)):
                engine.tensor_tensor(lo[layer][:, j], raw[layer][:, j], hi[layer][:, j].bitcast(f32), ALU.subtract).then_inc(w_lo_ok[layer][j], 1)

        def y_low(engine, wait_ge, c):
            if c >= 1:
                wait_ge(up_full, J * (BLOCKS.index((MIX, c - 1)) + 1))
            for f in range(KD):
                wait_ge(y_hi_ok, KD * c + f + 1)
                engine.tensor_tensor(y_lo[:, f, :], v_fm[:, f, :], y_hi[:, f, :].bitcast(f32), ALU.subtract).then_inc(y_lo_ok, 1)

        block = ctx.enter_context(nc.Block())

        @block.sync
        def _(sp):
            sp.dma_start(c_sb[:, :], c_d).then_inc(c_in, 16)
            sp.dma_start(wmod[:, :, 0:2 * D], wmod_d[:, :, 0:2 * D]).then_inc(wmod_in[0], 16)
            tok_v = x_d.rearrange("a (c t p) d -> p (a c) t d", p=P, t=TT)
            sp.dma_start(tok[:, 0], tok_v[:, 0]).then_inc(tok_in[0], 16)
            sp.dma_start(wqkv_raw[:, :, :, :], wqkv_d).then_inc(wqkv_in, 16)
            sp.dma_start(wmod[:, :, 2 * D:6 * D], wmod_d[:, :, 2 * D:6 * D]).then_inc(wmod_in[1], 16)
            sp.dma_start(tok[:, 1], tok_v[:, 1]).then_inc(tok_in[1], 16)
            half = J // 2
            for n in range(2):
                sp.dma_start(up_raw[MIX][:, n * half:(n + 1) * half], wmix_up_d[:, n * half:(n + 1) * half]).then_inc(up_in[MIX], 16)
            sp.dma_start(down_raw[MIX][:, :, :], wmix_out_d).then_inc(down_in[MIX], 16)
            for n in range(2):
                sp.dma_start(up_raw[FFN][:, n * half:(n + 1) * half], wffn_up_d[:, n * half:(n + 1) * half]).then_inc(up_in[FFN], 16)
            sp.dma_start(down_raw[FFN][:, :, :], wffn_down_d).then_inc(down_in[FFN], 16)
            for c in range(2, NC):
                sp.dma_start(tok[:, c], tok_v[:, c]).then_inc(tok_in[c], 16)
            out_v = out_d.rearrange("a (c t p) d -> p (a c) t d", p=P, t=TT)
            for c in range(NC):
                for f in range(2):
                    sp.wait_ge(tr_free[f], turn("back", BLOCKS.index((FFN, c))) + 1)
                    sp.dma_start(out_v[:, c, 2 * f:2 * f + 2], tok[:, c, 2 * f:2 * f + 2]).then_inc(stored, 16)
            sp.wait_ge(stored, 16 * 2 * NC)

        @block.tensor
        def _(pe):
            def modulation():
                pe.wait_ge(wide_ok, KD)
                pe.wait_ge(wmod_in[0], 16)
                for k in range(KD):
                    last = nc.tensor.matmul(gate_ps[0][:, :], silu_c_wide[:, k, :], wmod[:, k, 0:2 * D], start=k == 0, stop=k == KD - 1)
                last.then_inc(mod_ps_ok, 1)

            def modulation_gate():
                pe.wait_ge(wmod_in[1], 16)
                for k in range(KD):
                    last = nc.tensor.matmul(gate_ps[1][:, 0:D], silu_c_wide[:, k, :], wmod[:, k, 2 * D:3 * D], start=k == 0, stop=k == KD - 1)
                last.then_inc(mod_ps_ok, 1)

            def modulation_columns():
                for m in range(2, 6):
                    for f in range(KD):
                        for k in range(KD):
                            col = m * D + f * P
                            last = nc.tensor.matmul(up_ps[0][:, m * KD + f:m * KD + f + 1], wmod[:, k, col:col + P],
                                                    silu_c[:, k:k + 1], start=k == 0, stop=k == KD - 1)
                last.then_inc(mod_ps_ok, 1)

            def transit_transpose(what, which, src):
                n = turn(what, which)
                for f in range(KD):
                    if n >= 1:
                        pe.wait_ge(tr_free[f], n)
                    for t in range(TT):
                        last = nc.tensor.transpose(tr_ps[f][:, t * P:(t + 1) * P], src[:, t, f * P:(f + 1) * P], ident[:, :])
                    last.then_inc(tr_full[f], 1)

            def transit_h(c):
                pe.wait_ge(hs_ok, c + 1)
                transit_transpose("h", c, hs_tok)

            def transit_x(c):
                pe.wait_ge(x2_ok, c + 1)
                transit_transpose("x", c, x2_tok)

            def transit_back(b):
                n = turn("back", b)
                pe.wait_ge(out_taken, KD * (b + 1))
                for g in range(2):
                    pe.wait_ge(tr_free[g], n)
                    for u in range(2):
                        for f in range(KD):
                            col = (u * KD + f) * P
                            tt = 2 * g + u
                            last = nc.tensor.transpose(tr_ps[g][:, col:col + P], out_fm[:, f, tt * P:(tt + 1) * P], ident[:, :])
                    last.then_inc(tr_full[g], 1)

            def project(what, c):
                part = PARTS.index(what)
                n = turn(what, c)
                if what == "k":
                    for f in range(KD):
                        pe.wait_ge(tr_free[f], turn("h", c) + 1)
                if c == 0:
                    pe.wait_ge(wqkv_lo_ok, part + 1)
                for f in range(KD):
                    pe.wait_ge(tr_free[f], n)
                    cols_f = slice(f * P, (f + 1) * P)
                    for k in range(KD):
                        nc.tensor.matmul(tr_ps[f][:, :], wqkv_hi[:, part, k, cols_f], h_hi[:, k, :], start=k == 0, stop=False)
                        nc.tensor.matmul(tr_ps[f][:, :], wqkv_hi[:, part, k, cols_f], h_lo[:, k, :], start=False, stop=False)
                        last = nc.tensor.matmul(tr_ps[f][:, :], wqkv_lo[:, part, k, cols_f], h_hi[:, k, :], start=False, stop=k == KD - 1)
                    last.then_inc(tr_full[f], 1)

            def sums(c):
                n = turn("s", c)
                for f in range(2):
                    pe.wait_ge(ss_ok, 2 * c + f + 1)
                    pe.wait_ge(tr_free[f], n)
                    nc.tensor.matmul(tr_ps[f][:, :], ones_r[:, :], ss_hi[:, f, :], start=True, stop=False)
                    nc.tensor.matmul(tr_ps[f][:, :], ones_r[:, :], ss_lo[:, f, :], start=False, stop=True).then_inc(tr_full[f], 1)

            def hidden_tile(t):
                b, j = divmod(t, J)
                layer, c = BLOCKS[b]
                src_hi, src_lo = (y_hi, y_lo) if layer == MIX else (x2_hi, x2_lo)
                if j == 0:
                    pe.wait_ge(y_lo_ok if layer == MIX else x2_lo_ok, KD * (c + 1))
                if c == 0:
                    pe.wait_ge(w_lo_ok[layer][j], 1)
                hi, lo = up_hi[layer], up_lo[layer]
                for which, bank, taken, full in ((1, gate_ps[t % 2], silu_ok, gate_full), (0, up_ps[t % 2], hid_ok, up_full)):
                    if t >= 2:
                        pe.wait_ge(taken, t - 1)
                    for k in range(KD):
                        nc.tensor.matmul(bank[:, :], hi[:, j, k, which, :], src_hi[:, k, :], start=k == 0, stop=False)
                        nc.tensor.matmul(bank[:, :], hi[:, j, k, which, :], src_lo[:, k, :], start=False, stop=False)
                        last = nc.tensor.matmul(bank[:, :], lo[:, j, k, which, :], src_hi[:, k, :], start=False, stop=k == KD - 1)
                    last.then_inc(full, 1)

            def down_tile(t):
                b, j = divmod(t, J)
                layer, c = BLOCKS[b]
                pe.wait_ge(hid_lo_ok, t + 1)
                if c == 0:
                    pe.wait_ge(w_lo_ok[layer][j], 2)
                if j == 0 and b >= 1:
                    pe.wait_ge(out_taken, KD * b)
                hi, lo = down_hi[layer], down_lo[layer]
                s = t % HS_SLOTS
                for f in range(KD):
                    cols_f = slice(f * P, (f + 1) * P)
                    nc.tensor.matmul(out_ps[f][:, :], hi[:, j, cols_f], hid_hi[:, s, :], start=j == 0, stop=False)
                    nc.tensor.matmul(out_ps[f][:, :], hi[:, j, cols_f], hid_lo[:, s, :], start=False, stop=False)
                    last = nc.tensor.matmul(out_ps[f][:, :], lo[:, j, cols_f], hid_hi[:, s, :], start=False, stop=j == J - 1)
                last.then_inc(down_done, 1)

            modulation()
            pe.wait_ge(ident_ok, 1)
            transit_h(0)
            modulation_gate()
            for what in "kqv":
                project(what, 0)
            pe.wait_ge(ones_ok, 1)
            sums(0)
            modulation_columns()
            pe.wait_ge(cols_ok, 1)
            for t in range(NB * J):
                b, j = divmod(t, J)
                hidden_tile(t)
                if t >= LAG:
                    down_tile(t - LAG)
                if b == 0:
                    if j == 0:
                        transit_h(1)
                    if j == 1:
                        project("k", 1)
                        project("q", 1)
                    if j == 2:
                        project("v", 1)
                        sums(1)
                elif b in PROJECT_IN:
                    c = PROJECT_IN[b]
                    if j == 2:
                        transit_back(b - 1)
                    if j == 3:
                        transit_h(c)
                    if j in (4, 5):
                        project("kq"[j - 4], c)
                    if j == 6 and BLOCKS[b - 1][0] == MIX:
                        transit_x(BLOCKS[b - 1][1])
                    if j == 7:
                        project("v", c)
                elif b in SCAN_IN:
                    if j == 0:
                        sums(SCAN_IN[b])
                    if j == 4:
                        transit_back(b - 1)
                    if j == 7:
                        transit_x(BLOCKS[b - 1][1])
                else:
                    if j == 2:
                        transit_back(b - 1)
                    if j == 6 and BLOCKS[b - 1][0] == MIX:
                        transit_x(BLOCKS[b - 1][1])
            for t in range(NB * J - LAG, NB * J):
                down_tile(t)
            transit_back(NB - 1)

        @block.scalar
        def _(act):
            def take_h(c):
                n = turn("h", c)
                for f in range(KD):
                    act.wait_ge(tr_full[f], n + 1)
                    nc.scalar.activation(h_hi[:, f, :], tr_ps[f][:, :], ACT.Copy).then_inc(h_hi_ok, 1)

            def take_squares(what, c):
                dst, sq = (q_fm, sq_q) if what == "q" else (k_fm, k_squares(c))
                n = turn(what, c)
                if c >= 1 and what == "q":
                    act.wait_ge(y_ok, KD * c)
                if c >= 1 and what == "k":
                    act.wait_ge(y_ok, KD * c)
                    act.wait_ge(resid_ok, c + 1)
                for f in range(KD):
                    act.wait_ge(tr_full[f], n + 1)
                    nc.scalar.activation(dst[:, f, :], tr_ps[f][:, :], ACT.Copy).then_inc(qkv_ok, 1)
                    nc.scalar.activation(sq[:, f, :], tr_ps[f][:, :], ACT.Square).then_inc(tr_free[f], 1)

            def take_v(c):
                n = turn("v", c)
                if c >= 1:
                    act.wait_ge(y_lo_ok, KD * c)
                for f in range(KD):
                    act.wait_ge(tr_full[f], n + 1)
                    nc.scalar.activation(v_fm[:, f, :], tr_ps[f][:, :], ACT.Copy).then_inc(tr_free[f], 1)

            def rms_factors(c):
                n = turn("s", c)
                r_k = k_squares(c)[:, 0, :]
                for f, r, done in ((0, r_k, rk_ok), (1, r_q, rq_ok)):
                    act.wait_ge(tr_full[f], n + 1)
                    nc.scalar.activation(r, tr_ps[f][:, :], ACT.Ln, scale=1.0 / D, bias=eps_col[:, :]).then_inc(tr_free[f], 1)
                    act.wait_ge(tr_free[f], n + 1)
                    nc.scalar.activation(r, r, ACT.Exp, scale=-0.5).then_inc(done, 1)

            def exp_k(c):
                for f in range(KD):
                    act.wait_ge(kn_ok, KD * c + f + 1)
                    nc.scalar.activation(k_fm[:, f, :], k_fm[:, f, :], ACT.Exp).then_inc(w_ok, 1)

            def exp_q(c):
                for f in range(KD):
                    act.wait_ge(qn_ok, KD * c + f + 1)
                    nc.scalar.activation(q_fm[:, f, :], q_fm[:, f, :], ACT.Exp, scale=-1.0).then_inc(e_ok, 1)

            def recip_guess(c):
                for f in range(KD):
                    act.wait_ge(den_ok, KD * c + f + 1)
                    nc.scalar.activation(k_fm[:, f, :], q_fm[:, f, :], ACT.Ln).then_inc(ln_ok, 1)
                    act.wait_ge(ln_ok, KD * c + f + 1)
                    nc.scalar.activation(k_fm[:, f, :], k_fm[:, f, :], ACT.Exp, scale=-1.0).then_inc(guess_ok, 1)

            def y_high(c):
                if c >= 1:
                    act.wait_ge(up_full, J * (BLOCKS.index((MIX, c - 1)) + 1))
                for f in range(KD):
                    act.wait_ge(y_ok, KD * c + f + 1)
                    nc.scalar.activation(y_hi[:, f, :], v_fm[:, f, :], ACT.Copy).then_inc(y_hi_ok, 1)

            def h_squares(c):
                act.wait_ge(h_ok, c + 1)
                if c >= 1:
                    act.wait_ge(qn_ok, KD * c)
                for t in range(TT):
                    last = nc.scalar.activation(hs_tok[:, t, :], h_tok[:, t, :], ACT.Square, accum_out=h_sum[:, t:t + 1])
                last.then_inc(h_sum_ok, 1)

            def take_out(b):
                layer, c = BLOCKS[b]
                if b >= 1:
                    act.wait_ge(tr_full[1], turn("back", b - 1) + 1)
                    if BLOCKS[b - 1][0] == MIX:
                        act.wait_ge(x2_lo_ok, KD * (BLOCKS[b - 1][1] + 1))
                act.wait_ge(down_done, J * (b + 1))
                gate = cols[:, 2 if layer == MIX else 5, :]
                for f in range(KD):
                    nc.scalar.activation(out_fm[:, f, :], out_ps[f][:, :], ACT.Copy, scale=gate[:, f:f + 1]).then_inc(out_taken, 1)

            def take_x(c):
                n = turn("x", c)
                for f in range(KD):
                    act.wait_ge(tr_full[f], n + 1)
                    nc.scalar.activation(x2_fm[:, f, :], tr_ps[f][:, :], ACT.Identity, scale=cols[:, 4, f:f + 1],
                                         bias=cols[:, 3, f:f + 1]).then_inc(tr_free[f], 1)
                if c >= 1:
                    act.wait_ge(up_full, J * (BLOCKS.index((FFN, c - 1)) + 1))
                for f in range(KD):
                    act.wait_ge(tr_free[f], n + 1)
                    nc.scalar.activation(x2_hi[:, f, :], x2_fm[:, f, :], ACT.Copy).then_inc(x2_hi_ok, 1)

            def split_hi(layer, j):
                nc.scalar.activation(up_hi[layer][:, j], up_raw[layer][:, j], ACT.Copy).then_inc(w_hi_ok[layer], 1)
                nc.scalar.activation(down_hi[layer][:, j], down_raw[layer][:, j], ACT.Copy).then_inc(w_hi_ok[layer], 1)

            def silu_tile(t):
                act.wait_ge(gate_full, t + 1)
                if t >= 2:
                    act.wait_ge(hid_lo_ok, t - 1)
                nc.scalar.activation(hid[:, t % 2, :], gate_ps[t % 2][:, :], ACT.Silu).then_inc(silu_ok, 1)

            def hi_tile(t):
                act.wait_ge(hid_ok, t + 1)
                if t >= HS_SLOTS:
                    act.wait_ge(down_done, t - HS_SLOTS + 1)
                nc.scalar.activation(hid_hi[:, t % HS_SLOTS, :], hid[:, t % 2, :], ACT.Copy).then_inc(hid_hi_ok, 1)

            act.wait_ge(c_in, 16)
            nc.scalar.activation(silu_c[:, :], c_sb[:, :], ACT.Silu).then_inc(silu_c_ok, 1)
            nc.scalar.preload_act_table_set(LN_EXP)
            act.wait_ge(consts, 1)
            h_squares(0)
            act.wait_ge(wqkv_in, 16)
            for part in range(3):
                nc.scalar.activation(wqkv_hi[:, part], wqkv_raw[:, part], ACT.Copy).then_inc(wqkv_hi_ok, 1)
            take_h(0)
            take_squares("k", 0)
            take_squares("q", 0)
            take_v(0)
            rms_factors(0)
            exp_k(0)
            exp_q(0)
            act.wait_ge(up_in[MIX], 32)
            act.wait_ge(down_in[MIX], 16)
            for j in range(J // 2):
                split_hi(MIX, j)
            recip_guess(0)
            nc.scalar.preload_act_table_set(SILU)
            y_high(0)
            h_squares(1)
            for j in range(J // 2, J):
                split_hi(MIX, j)
            act.wait_ge(cols_ok, 1)
            for t in range(NB * J + 1):
                b, j = divmod(t, J)
                if t < NB * J:
                    silu_tile(t)
                if t >= 1:
                    hi_tile(t - 1)
                if b == NB:
                    break
                if b == 0:
                    if j == 0:
                        take_h(1)
                    if j == 1:
                        take_squares("k", 1)
                        take_squares("q", 1)
                    if j == 2:
                        take_v(1)
                if b in SCAN_IN:
                    if j == SCAN_AT[b]:
                        nc.scalar.preload_act_table_set(LN_EXP)
                        rms_factors(SCAN_IN[b])
                    if j == SCAN_AT[b] + 1:
                        nc.scalar.preload_act_table_set(LN_EXP)
                        exp_k(SCAN_IN[b])
                        exp_q(SCAN_IN[b])
                    if j == SCAN_AT[b] + 3:
                        nc.scalar.preload_act_table_set(LN_EXP)
                        recip_guess(SCAN_IN[b])
                    if j in (SCAN_AT[b], SCAN_AT[b] + 1, SCAN_AT[b] + 3):
                        nc.scalar.preload_act_table_set(SILU)
                    if j == SCAN_AT[b] + 4:
                        y_high(SCAN_IN[b])
                if b == 0:
                    continue
                if j == 0 and b - 1 in SCAN_IN and b >= 2:
                    take_x(BLOCKS[b - 2][1])
                if j == 1:
                    take_out(b - 1)
                if b == 1:
                    if j == 0:
                        act.wait_ge(up_in[FFN], 32)
                        act.wait_ge(down_in[FFN], 16)
                    split_hi(FFN, j)
                if b in PROJECT_IN:
                    c = PROJECT_IN[b]
                    if j == 2:
                        h_squares(c)
                    if j == 3:
                        take_h(c)
                    if j in (4, 5):
                        take_squares("kq"[j - 4], c)
                    if j == 7:
                        take_v(c)
                if b not in SCAN_IN and j == 6 and BLOCKS[b - 1][0] == MIX:
                    take_x(BLOCKS[b - 1][1])
            take_out(NB - 1)

        @block.vector
        def _(dve):
            steps = [0]

            def link(ins):
                steps[0] += 1
                ins.then_inc(dve_step, 1)
                dve.wait_ge(dve_step, steps[0])

            def token_stats(src, st, mv, done):
                for t in range(TT):
                    last = nc.vector.bn_stats(st[:, t, :], src[:, t, :])
                link(last)
                for t in range(TT):
                    last = nc.vector.bn_aggr(mv[:, t, :], st[:, t, :])
                last.then_inc(done, 1)

            def normalise(dst, src, mv, rs, rs_ok, n, done):
                dve.wait_ge(rs_ok, n)
                for t in range(TT):
                    last = nc.vector.tensor_scalar(dst[:, t, :], src[:, t, :], mv[:, t, 0:1], rs[:, t:t + 1], ALU.subtract, ALU.mult)
                last.then_inc(done, 1)

            def ln1_stats(c):
                dve.wait_ge(tok_in[c], 16)
                token_stats(tok[:, c], stats, mean_var, stats_ok)

            def ln1_normalise(c):
                dve.wait_ge(resid_ok, c)
                if c >= 2:
                    dve.wait_ge(kn_ok, KD * c)
                normalise(h_tok, tok[:, c], mean_var, rstd, rstd_ok, c + 1, norm_ok)

            def take_h(c):
                for f in range(KD):
                    dve.wait_ge(h_hi_ok, KD * c + f + 1)
                    nc.vector.tensor_tensor(h_lo[:, f, :], tr_ps[f][:, :], h_hi[:, f, :].bitcast(f32), ALU.subtract).then_inc(tr_free[f], 1)

            def k_norm(c):
                dve.wait_ge(rk_ok, c + 1)
                r_k = k_squares(c)[:, 0, :]
                for f in range(KD):
                    nc.vector.tensor_tensor(k_fm[:, f, :], k_fm[:, f, :], r_k, ALU.mult).then_inc(kn_ok, 1)

            def scan(c, f):
                dve.wait_ge(w_ok, KD * c + f + 1)
                link(nc.vector.tensor_tensor(v_fm[:, f, :], v_fm[:, f, :], k_fm[:, f, :], ALU.mult))
                link(nc.vector.tensor_tensor_scan(k_fm[:, f, :], one_col[:, :].to_broadcast([P, CH]), k_fm[:, f, :],
                                                  carry[:, 0, f:f + 1], ALU.mult, ALU.add))
                link(nc.vector.tensor_tensor_scan(v_fm[:, f, :], one_col[:, :].to_broadcast([P, CH]), v_fm[:, f, :],
                                                  carry[:, 1, f:f + 1], ALU.mult, ALU.add))
                nc.vector.tensor_copy(carry[:, 0, f:f + 1], k_fm[:, f, CH - 1:CH])
                link(nc.vector.tensor_copy(carry[:, 1, f:f + 1], v_fm[:, f, CH - 1:CH]))

            def denominator(c, f):
                dve.wait_ge(e_ok, KD * c + f + 1)
                nc.vector.scalar_tensor_tensor(out=q_fm[:, f, :], in0=q_fm[:, f, :], scalar=1.0, in1=k_fm[:, f, :],
                                               op0=ALU.add, op1=ALU.mult).then_inc(den_ok, 1)

            def reciprocal(c, f):
                dve.wait_ge(guess_ok, KD * c + f + 1)
                link(nc.vector.tensor_tensor(q_fm[:, f, :], q_fm[:, f, :], k_fm[:, f, :], ALU.mult))
                link(nc.vector.scalar_tensor_tensor(out=q_fm[:, f, :], in0=q_fm[:, f, :], scalar=-2.0, in1=k_fm[:, f, :],
                                                    op0=ALU.add, op1=ALU.mult))
                nc.vector.scalar_tensor_tensor(out=v_fm[:, f, :], in0=v_fm[:, f, :], scalar=-1.0, in1=q_fm[:, f, :],
                                               op0=ALU.mult, op1=ALU.mult).then_inc(y_ok, 1)

            def take_back(b):
                layer, c = BLOCKS[b]
                n = turn("back", b)
                if layer == MIX:
                    dve.wait_ge(resid_ok, c + 1)
                for g in range(2):
                    dve.wait_ge(tr_full[g], n + 1)
                    rows = tok[:, c, 2 * g:2 * g + 2, :].rearrange("p t d -> p (t d)")
                    nc.vector.tensor_tensor(rows, tr_ps[g][:, :], rows, ALU.add).then_inc(tr_free[g], 1)
                if layer == FFN:
                    return
                for g in range(2):
                    dve.wait_ge(tr_free[g], n + 1)
                token_stats(tok[:, c], stats2, mean_var2, stats2_ok)
                if c >= 1:
                    for f in range(KD):
                        dve.wait_ge(tr_full[f], turn("x", c - 1) + 1)
                normalise(x2_tok, tok[:, c], mean_var2, rstd2, rstd2_ok, c + 1, x2_ok)

            def take_x(c):
                for f in range(KD):
                    dve.wait_ge(x2_hi_ok, KD * c + f + 1)
                    nc.vector.tensor_tensor(x2_lo[:, f, :], x2_fm[:, f, :], x2_hi[:, f, :].bitcast(f32), ALU.subtract).then_inc(x2_lo_ok, 1)

            def mul_tile(t):
                dve.wait_ge(silu_ok, t + 1)
                dve.wait_ge(up_full, t + 1)
                nc.vector.tensor_tensor(hid[:, t % 2, :], up_ps[t % 2][:, :], hid[:, t % 2, :], ALU.mult).then_inc(hid_ok, 1)

            def lo_tile(t):
                dve.wait_ge(hid_hi_ok, t + 1)
                s = t % HS_SLOTS
                nc.vector.tensor_tensor(hid_lo[:, s, :], hid[:, t % 2, :], hid_hi[:, s, :].bitcast(f32), ALU.subtract).then_inc(hid_lo_ok, 1)

            nc.vector.memset(one_col[:, :], 1.0)
            nc.vector.memset(eps_col[:, :], RMS_EPS)
            nc.vector.memset(carry[:, 0, :], CUM_EPS)
            nc.vector.memset(carry[:, 1, :], 0.0)
            nc.vector.memset(ones_r[:, :].bitcast(f32), 1.0).then_inc(ones_ok, 1)
            link(nc.vector.memset(ones[:, :], 1.0))
            nc.vector.memset(minus_half[:, :], -0.5).then_inc(consts, 1)
            dve.wait_ge(silu_c_ok, 1)
            for k in range(KD):
                nc.vector.tensor_scalar(silu_c_wide[:, k, :], ones[:, :], silu_c[:, k:k + 1], None, ALU.mult).then_inc(wide_ok, 1)
            dve.wait_ge(tok_in[0], 16)
            token_stats(tok[:, 0], stats, mean_var, stats_ok)
            dve.wait_ge(mod_ps_ok, 1)
            nc.vector.tensor_copy(mod_shift[:, :], gate_ps[0][:, 0:D])
            link(nc.vector.tensor_scalar(mod_scale[:, :], gate_ps[0][:, D:2 * D], 1.0, None, ALU.add))
            normalise(h_tok, tok[:, 0], mean_var, rstd, rstd_ok, 1, norm_ok)
            dve.wait_ge(norm_ok, 1)
            wide = mod_scale[:, :].unsqueeze(1).to_broadcast([P, TT, D])
            link(nc.vector.tensor_tensor(h_tok[:, :, :], h_tok[:, :, :], wide, ALU.mult))
            wide = mod_shift[:, :].unsqueeze(1).to_broadcast([P, TT, D])
            nc.vector.tensor_tensor(h_tok[:, :, :], h_tok[:, :, :], wide, ALU.add).then_inc(h_ok, 1)
            dve.wait_ge(h_rms_ok, 1)
            for t in range(TT):
                last = nc.vector.tensor_scalar(hs_tok[:, t, :], h_tok[:, t, :], h_rms[:, t:t + 1], None, ALU.mult)
            last.then_inc(hs_ok, 1)
            for part in range(3):
                dve.wait_ge(wqkv_hi_ok, part + 1)
                nc.vector.tensor_tensor(wqkv_lo[:, part], wqkv_raw[:, part], wqkv_hi[:, part].bitcast(f32), ALU.subtract).then_inc(wqkv_lo_ok, 1)
            take_h(0)
            def gate_of(dst, src, tmp):
                link(nc.vector.tensor_scalar(tmp, src, 0.0, 2.0, ALU.is_ge, ALU.mult))
                link(nc.vector.tensor_scalar(dst, src, GATE_MIN, None, ALU.max))
                link(nc.vector.scalar_tensor_tensor(out=dst, in0=src, scalar=-1.0, in1=dst, op0=ALU.mult, op1=ALU.max))
                return nc.vector.scalar_tensor_tensor(out=dst, in0=tmp, scalar=-1.0, in1=dst, op0=ALU.add, op1=ALU.mult)

            dve.wait_ge(mod_ps_ok, 2)
            gate_of(gate_tok[:, :], gate_ps[1][:, 0:D], out_fm[:, 0, 0:D]).then_inc(mod_ok, 1)
            ln1_stats(1)
            sums_of_squares(nc.vector, dve.wait_ge, link, 0)
            ln1_normalise(1)
            k_norm(0)
            for f in range(KD):
                scan(0, f)
                denominator(0, f)
            dve.wait_ge(mod_ps_ok, 3)
            col_ps = up_ps[0][:, 0:6 * KD].rearrange("p (m f) -> p m f", f=KD)
            link(gate_of(cols[:, 2, :], col_ps[:, 2, :], col_t[:, 0, :]))
            link(gate_of(cols[:, 5, :], col_ps[:, 5, :], col_t[:, 1, :]))
            nc.vector.tensor_copy(cols[:, 3, :], col_ps[:, 3, :])
            nc.vector.tensor_scalar(cols[:, 4, :], col_ps[:, 4, :], 1.0, None, ALU.add).then_inc(cols_ok, 1)
            for f in range(KD):
                reciprocal(0, f)
            y_low(nc.vector, dve.wait_ge, 0)
            for t in range(NB * J + 1):
                b, j = divmod(t, J)
                if t < NB * J:
                    mul_tile(t)
                if t >= 1:
                    lo_tile(t - 1)
                if b == NB:
                    break
                if b in SCAN_IN:
                    c = SCAN_IN[b]
                    if b == 0 and j == 0:
                        take_h(c)
                    if b == 0 and j == 1:
                        sums_of_squares(nc.vector, dve.wait_ge, link, c)
                    if j == SCAN_AT[b]:
                        k_norm(c)
                    for f in range(KD):
                        if j == SCAN_AT[b] + 1 + f:
                            scan(c, f)
                            denominator(c, f)
                        if j == SCAN_AT[b] + 3:
                            reciprocal(c, f)
                if b == 0:
                    if j < 4:
                        split_lo(nc.vector, dve.wait_ge, MIX, j + 4)
                    continue
                if j == 0 and b - 1 in SCAN_IN and b >= 2:
                    take_x(BLOCKS[b - 2][1])
                if b in PROJECT_IN:
                    if j == 0:
                        ln1_stats(PROJECT_IN[b])
                        ln1_normalise(PROJECT_IN[b])
                    if j == 3:
                        take_h(PROJECT_IN[b])
                if j == (6 if b in SCAN_IN else 2):
                    take_back(b - 1)
                if b not in SCAN_IN and j == 6 and BLOCKS[b - 1][0] == MIX:
                    take_x(BLOCKS[b - 1][1])
            take_back(NB - 1)

        @block.gpsimd
        def _(pool):
            steps = [0]

            def link(ins):
                steps[0] += 1
                ins.then_inc(pool_step, 1)
                pool.wait_ge(pool_step, steps[0])

            def power_of(dst, src, by, plus, done):
                link(nc.gpsimd.tensor_scalar(dst, src, by, plus, ALU.mult, ALU.add))
                nc.gpsimd.tensor_tensor(dst, dst, minus_half[:, :], ALU.pow).then_inc(done, 1)

            def token_rstd(c):
                pool.wait_ge(stats_ok, c + 1)
                power_of(rstd[:, :], mean_var[:, :, 1], 1.0, LN_EPS, rstd_ok)

            def token_rstd2(c):
                pool.wait_ge(stats2_ok, c + 1)
                power_of(rstd2[:, :], mean_var2[:, :, 1], 1.0, LN_EPS, rstd2_ok)

            def token_rms(c):
                pool.wait_ge(h_sum_ok, c + 1)
                power_of(h_rms[:, :], h_sum[:, :], 1.0 / D, RMS_EPS, h_rms_ok)

            def modulate(c):
                pool.wait_ge(norm_ok, c + 1)
                wide = mod_scale[:, :].unsqueeze(1).to_broadcast([P, TT, D])
                link(nc.gpsimd.tensor_tensor(h_tok[:, :, :], h_tok[:, :, :], wide, ALU.mult))
                wide = mod_shift[:, :].unsqueeze(1).to_broadcast([P, TT, D])
                nc.gpsimd.tensor_tensor(h_tok[:, :, :], h_tok[:, :, :], wide, ALU.add).then_inc(h_ok, 1)

            def scale_by_rms(c):
                pool.wait_ge(h_rms_ok, c + 1)
                for t in range(TT):
                    last = nc.gpsimd.tensor_scalar(hs_tok[:, t, :], h_tok[:, t, :], h_rms[:, t:t + 1], 0.0, ALU.mult, ALU.add)
                last.then_inc(hs_ok, 1)

            def residual(c):
                pool.wait_ge(mod_ok, 1)
                pool.wait_ge(hs_ok, c + 1)
                wide = gate_tok[:, :].unsqueeze(1).to_broadcast([P, TT, D])
                link(nc.gpsimd.tensor_tensor(h_tok[:, :, :], h_tok[:, :, :], wide, ALU.mult))
                nc.gpsimd.tensor_tensor(tok[:, c], tok[:, c], h_tok[:, :, :], ALU.add).then_inc(resid_ok, 1)

            def q_norm(c):
                pool.wait_ge(rq_ok, c + 1)
                for f in range(KD):
                    nc.gpsimd.tensor_tensor(q_fm[:, f, :], q_fm[:, f, :], r_q, ALU.mult).then_inc(qn_ok, 1)

            link(nc.gpsimd.memset(ident[:, :], 0.0))
            nc.gpsimd.affine_select(out=ident[:, :], in_=ident[:, :], compare_op=ALU.not_equal, fill=1.0, base=0,
                                    pattern=[[-1, P]], channel_multiplier=1).then_inc(ident_ok, 1)
            pool.wait_ge(consts, 1)
            token_rstd(0)
            token_rms(0)
            residual(0)
            token_rstd(1)
            q_norm(0)
            split_lo(nc.gpsimd, pool.wait_ge, MIX, 0)
            modulate(1)
            split_lo(nc.gpsimd, pool.wait_ge, MIX, 1)
            split_lo(nc.gpsimd, pool.wait_ge, MIX, 2)
            token_rms(1)
            scale_by_rms(1)
            split_lo(nc.gpsimd, pool.wait_ge, MIX, 3)
            residual(1)
            for b in range(NB):
                if b in PROJECT_IN:
                    c = PROJECT_IN[b]
                    token_rstd(c)
                    modulate(c)
                    token_rms(c)
                    scale_by_rms(c)
                    if BLOCKS[b - 1][0] == MIX:
                        token_rstd2(BLOCKS[b - 1][1])
                    residual(c)
                    if b == 1:
                        for j in range(4):
                            split_lo(nc.gpsimd, pool.wait_ge, FFN, j)
                    sums_of_squares(nc.gpsimd, pool.wait_ge, link, c)
                    if b == 1:
                        for j in range(4, J):
                            split_lo(nc.gpsimd, pool.wait_ge, FFN, j)
                elif b in SCAN_IN:
                    q_norm(SCAN_IN[b])
                    y_low(nc.gpsimd, pool.wait_ge, SCAN_IN[b])
                if b not in PROJECT_IN and b >= 1 and BLOCKS[b - 1][0] == MIX:
                    token_rstd2(BLOCKS[b - 1][1])


def kernel(L0_attn_x, L0_attn_w_qkv, L0_attn_w_swiglu, L0_attn_w_out, L0_ffn_w_gate, L0_ffn_w_up, L0_ffn_w_down, L0_c, L0_wmod):
    import numpy as np
    import concourse.bacc as bacc
    from concourse.bass_utils import run_bass_kernel_spmd

    def lay(a, shape, order):
        return np.ascontiguousarray(np.asarray(a).reshape(shape).transpose(order))

    arrays = {
        "x": np.ascontiguousarray(L0_attn_x),
        "c": lay(L0_c, (KD, P), (1, 0)),
        "wmod": lay(L0_wmod, (KD, P, 6 * D), (1, 0, 2)),
        "wqkv": lay(np.asarray(L0_attn_w_qkv).reshape(3, D, D)[[1, 0, 2]], (3, D, KD, P), (3, 0, 2, 1)),
        "wmix_up": lay(L0_attn_w_swiglu, (2, J, P, KD, P), (4, 1, 3, 0, 2)),
        "wmix_out": lay(L0_attn_w_out, (D, J, P), (2, 1, 0)),
        "wffn_up": lay(np.stack([np.asarray(L0_ffn_w_up), np.asarray(L0_ffn_w_gate)]), (2, J, P, KD, P), (4, 1, 3, 0, 2)),
        "wffn_down": lay(L0_ffn_w_down, (D, J, P), (2, 1, 0)),
    }
    nc = bacc.Bacc("TRN2", target_bir_lowering=False, num_devices=1)
    f32 = mybir.dt.float32
    ins = [nc.dram_tensor(n, a.shape, f32, kind="ExternalInput").ap() for n, a in arrays.items()]
    out = nc.dram_tensor("out", (1, S, D), f32, kind="ExternalOutput").ap()
    adaln_kernel(nc, *ins, out)
    return run_bass_kernel_spmd(nc, [arrays], core_ids=[0]).results[0]["out"]
```

```python
import concourse.bass as bass
from concourse import mybir
from contextlib import ExitStack

P = 128
S, D, F = 2048, 256, 1024
CH = 512
NC = S // CH
TT = CH // P
KD = D // P
J = F // P
LN_EPS = 1e-05
RMS_EPS = 1.1920929e-07
CUM_EPS = 1e-06
GATE_MIN = 0.25

MIX, FFN = 0, 1
BLOCKS = [(MIX, 0)]
for _c in range(NC - 1):
    BLOCKS += [(MIX, _c + 1), (FFN, _c)]
BLOCKS.append((FFN, NC - 1))
NB = len(BLOCKS)
LN_EXP, SILU = "natural_log_exp_and_others", "silu_and_others"
LAG = 2
HS_SLOTS = LAG + 1

PROJECT_IN = {1: 2, 3: 3}
SCAN_IN = {0: 1, 2: 2, 4: 3}
SCAN_AT = {0: 2, 2: 2, 4: 2}

TRANSIT = [(w, 0) for w in "hkqv"] + [(w, 1) for w in "hkvs"]
for _b in range(1, NB + 1):
    _x = [("x", BLOCKS[_b - 1][1])] * (BLOCKS[_b - 1][0] == MIX)
    if _b - 1 in SCAN_IN and _b > 1:
        TRANSIT.append(("x", BLOCKS[_b - 2][1]))
    if _b in PROJECT_IN:
        TRANSIT += [("back", _b - 1)] + [(w, PROJECT_IN[_b]) for w in "hkq"] + _x + [("v", PROJECT_IN[_b])]
    elif _b in SCAN_IN:
        TRANSIT += [("s", SCAN_IN[_b]), ("back", _b - 1)]
    else:
        TRANSIT += [("back", _b - 1)] + _x


def split_early(t):
    b, j = divmod(t, J)
    return b in SCAN_IN and j in (SCAN_AT[b], SCAN_AT[b] + 1, SCAN_AT[b] + 2)


PARTS = "kqv"


def turn(what, which):
    return TRANSIT.index((what, which))


def adaln_kernel(nc, x_d, c_d, wmod_d, wqkv_d, wmix_up_d, wmix_out_d, wffn_up_d, wffn_down_d, out_d):
    f32, f32r = mybir.dt.float32, mybir.dt.float32r
    ACT, ALU = mybir.ActivationFunctionType, mybir.AluOpType
    ctx = ExitStack()
    with ctx:
        at = [(nc.sbuf_base + 63) // 64 * 64]
        names = {}

        def place(name, shape, dt, offset=None):
            size = 4
            for n in shape[1:]:
                size *= n
            if offset is None:
                offset = at[0]
                at[0] += (size + 31) // 32 * 32
                assert at[0] <= nc.sbuf_usable_end, (name, at[0])
            names[name] = offset
            return nc.alloc_sbuf_tensor_at(name, shape, dt, offset=offset)

        def split_pair(name, shape):
            hi = place(name + "_hi", shape, f32r)
            lo = place(name + "_lo", shape, f32r)
            return hi, lo, place(name + "_raw", shape, f32, offset=names[name + "_lo"])

        wqkv_hi, wqkv_lo, wqkv_raw = split_pair("wqkv", [P, 3, KD, D])
        up_hi, up_lo, up_raw, down_hi, down_lo, down_raw = ([None, None] for _ in range(6))
        for layer, name in ((MIX, "mix"), (FFN, "ffn")):
            up_hi[layer], up_lo[layer], up_raw[layer] = split_pair(name + "_up", [P, J, KD, 2, P])
            down_hi[layer], down_lo[layer], down_raw[layer] = split_pair(name + "_down", [P, J, D])

        tok = place("tok", [P, NC, TT, D], f32)
        h_tok = place("h_tok", [P, TT, D], f32)
        hs_tok = place("hs_tok", [P, TT, D], f32)
        x2_tok = place("x2_tok", [P, TT, D], f32)
        out_fm = place("out_fm", [P, KD, CH], f32)
        x2_fm = place("x2_fm", [P, KD, CH], f32, offset=names["out_fm"])
        h_hi, h_lo = (place(n, [P, KD, CH], f32r) for n in ("h_hi", "h_lo"))
        y_hi, y_lo = ([place(f"{n}{slot}", [P, KD, CH], f32r) for slot in range(2)] for n in ("y_hi", "y_lo"))
        x2_hi, x2_lo = (place(n, [P, KD, CH], f32r) for n in ("x2_hi", "x2_lo"))
        q_fm, k_fm, v_fm = (place(n, [P, KD, CH], f32) for n in ("q_fm", "k_fm", "v_fm"))
        sq_q = place("sq_q", [P, KD, CH], f32, offset=names["hs_tok"])
        sq_k = place("sq_k", [P, KD, CH], f32, offset=names["h_tok"])
        sq_k0 = place("sq_k0", [P, KD, CH], f32, offset=names["x2_tok"])
        sq_q0 = place("sq_q0", [P, KD, CH], f32, offset=names["y_hi1"])
        ss_hi = [place(f"ss_hi{n}", [P, CH], f32r, offset=names[under] + CH * 4) for n, under in enumerate(("h_tok", "hs_tok"))]
        ss_lo = [place(f"ss_lo{n}", [P, CH], f32r, offset=names[under]) for n, under in enumerate(("h_tok", "hs_tok"))]
        hid = place("hid", [P, 2, CH], f32)
        hid_hi = place("hid_hi", [P, HS_SLOTS, CH], f32r)
        hid_lo = place("hid_lo", [P, HS_SLOTS, CH], f32r)
        wmod = place("wmod", [P, KD, 6 * D], f32, offset=names["hid_hi"])
        assert names["hid_lo"] == names["hid_hi"] + HS_SLOTS * CH * 4 and KD * 6 * D == 2 * HS_SLOTS * CH
        mod_scale, mod_shift, gate_tok = (place(n, [P, D], f32) for n in ("mod_scale", "mod_shift", "gate_tok"))
        ident = place("ident", [P, P], f32)
        ones_r = place("ones_r", [P, P], f32r)
        ones = place("ones", [P, P], f32, offset=names["x2_hi"])
        silu_c = place("silu_c", [P, KD], f32)
        silu_c_wide = place("silu_c_wide", [P, KD, P], f32, offset=names["x2_lo"])
        c_sb = place("c_sb", [P, KD], f32)
        cols = place("cols", [P, 6, KD], f32)
        col_sb = place("col_sb", [P, 6 * KD], f32)
        col_t = place("col_t", [P, 2, KD], f32)
        stats = place("stats", [P, TT, 6], f32)
        mean_var = place("mean_var", [P, TT, 2], f32)
        rstd = place("rstd", [P, TT], f32)
        stats2 = place("stats2", [P, TT, 6], f32)
        mean_var2 = place("mean_var2", [P, TT, 2], f32)
        rstd2 = place("rstd2", [P, TT], f32)
        h_sum = place("h_sum", [P, TT], f32)
        h_rms = place("h_rms", [P, TT], f32)
        minus_half = place("minus_half", [P, TT], f32)
        one_col = place("one_col", [P, 1], f32)
        eps_col = place("eps_col", [P, 1], f32)
        ln_eps_col = place("ln_eps_col", [P, 1], f32)
        carry = place("carry", [P, 2, KD], f32)

        def pb(name):
            return ctx.enter_context(nc.psum_tensor(name, [P, CH], f32))

        gate_ps = [pb(f"gate_ps{n}") for n in range(2)]
        up_ps = [pb(f"up_ps{n}") for n in range(2)]
        out_ps = [pb(f"out_ps{n}") for n in range(KD)]
        tr_ps = [pb(f"tr_ps{n}") for n in range(2)]

        def squares(what, c):
            return (sq_k0 if c == 0 else sq_k) if what == "k" else (sq_q0 if c == 0 else sq_q)

        def sem(name):
            return ctx.enter_context(nc.semaphore(name))

        c_in, wqkv_in = sem("c_in"), sem("wqkv_in")
        wmod_in = [sem(f"wmod_in{n}") for n in range(4)]
        tok_first_in = [sem(f"tok_first_in{n}") for n in range(2)]
        tok_in = [sem(f"tok_in{n}") for n in range(NC)]
        w_first_in = sem("w_first_in")
        w_in = [sem(f"w_in{layer}") for layer in (MIX, FFN)]
        consts, ident_ok, ones_ok = sem("consts"), sem("ident_ok"), sem("ones_ok")
        silu_c_ok, wide_ok = sem("silu_c_ok"), sem("wide_ok")
        mod_ps_ok, mod_ok, col_sb_ok, cols_ok = (sem(n) for n in ("mod_ps_ok", "mod_ok", "col_sb_ok", "cols_ok"))
        col_ps_ok = sem("col_ps_ok")
        last_half = sem("last_half")
        early_full, early_free = sem("early_full"), sem("early_free")
        dve_step, pool_step, act_step = sem("dve_step"), sem("pool_step"), sem("act_step")
        wqkv_hi_ok, wqkv_lo_ok = sem("wqkv_hi_ok"), sem("wqkv_lo_ok")
        w_hi_ok = [sem(f"w_hi_ok{layer}") for layer in (MIX, FFN)]
        w_lo_ok = [[sem(f"w_lo_ok{layer}_{j}") for j in range(J)] for layer in (MIX, FFN)]
        stats_ok, rstd_ok, norm_ok = sem("stats_ok"), sem("rstd_ok"), sem("norm_ok")
        h_ok, h_sum_ok, h_rms_ok, hs_ok = sem("h_ok"), sem("h_sum_ok"), sem("h_rms_ok"), sem("hs_ok")
        gated_ok = sem("gated_ok")
        resid_ok = sem("resid_ok")
        tr_full = [sem(f"tr_full{n}") for n in range(2)]
        tr_free = [sem(f"tr_free{n}") for n in range(2)]
        h_hi_ok, ss_ok = sem("h_hi_ok"), sem("ss_ok")
        rk_ok, rq_ok, w_ok, e_ok, q_sum_ok = (sem(n) for n in ("rk_ok", "rq_ok", "w_ok", "e_ok", "q_sum_ok"))
        kn_ok, qn_ok = ([sem(f"{n}{f}") for f in range(KD)] for n in ("kn_ok", "qn_ok"))
        ng_ok = sem("ng_ok")
        den_ok, ln_ok, guess_ok = sem("den_ok"), sem("ln_ok"), sem("guess_ok")
        y_ok, y_hi_ok, y_lo_ok = (sem(n) for n in ("y_ok", "y_hi_ok", "y_lo_ok"))
        gate_full, up_full, silu_ok, hid_ok, hid_hi_ok, hid_lo_ok, down_done = (
            sem(n) for n in ("gate_full", "up_full", "silu_ok", "hid_ok", "hid_hi_ok", "hid_lo_ok", "down_done"))
        out_taken, x2_ok, stats2_ok, rstd2_ok = sem("out_taken"), sem("x2_ok"), sem("stats2_ok"), sem("rstd2_ok")
        x2_hi_ok, x2_lo_ok, stored = sem("x2_hi_ok"), sem("x2_lo_ok"), sem("stored")

        def early(what, c):
            return (what, c) == ("q", 1)

        def arrived(what, c, f):
            return (early_full, KD + f + 1) if early(what, c) else (tr_full[f], turn(what, c) + 1)

        def taken(what, c, f):
            return (early_free, KD + f + 1) if early(what, c) else (tr_free[f], turn(what, c) + 1)

        def h_ok_at(c, t=TT - 1):
            return TT * c + t + 1 if c < 2 else TT * 2 + c - 1


        def norm(engine, wait_ge, what, c, f):
            wait_ge(rk_ok if what == "k" else rq_ok, c + 1)
            dst, r, done = (k_fm, squares("k", c)[:, 0, :], kn_ok) if what == "k" else (q_fm, squares("q", c)[:, 0, :], qn_ok)
            engine.tensor_tensor(dst[:, f, :], dst[:, f, :], r, ALU.mult).then_inc(done[f], 1)

        def sums_of_squares(engine, wait_ge, link, c):
            for n, what in enumerate("kq"):
                sq = squares(what, c)
                for f in range(KD):
                    wait_ge(*taken(what, c, f))
                link(engine.tensor_tensor(sq[:, 0, :], sq[:, 0, :], sq[:, 1, :], ALU.add))
                link(engine.tensor_scalar(ss_hi[n][:, :], sq[:, 0, :], 1.0, 0.0, ALU.mult, ALU.add))
                engine.tensor_tensor(ss_lo[n][:, :], sq[:, 0, :], ss_hi[n][:, :].bitcast(f32), ALU.subtract).then_inc(ss_ok, 1)

        def split_lo(engine, wait_ge, layer, j):
            wait_ge(w_hi_ok[layer], 2 * j + 2)
            for hi, lo, raw in ((up_hi, up_lo, up_raw), (down_hi, down_lo, down_raw)):
                engine.tensor_tensor(lo[layer][:, j], raw[layer][:, j], hi[layer][:, j].bitcast(f32), ALU.subtract).then_inc(w_lo_ok[layer][j], 1)

        def y_low(engine, wait_ge, c):
            if c >= 2:
                wait_ge(up_full, J * (BLOCKS.index((MIX, c - 2)) + 1))
            for f in range(KD):
                wait_ge(y_hi_ok, KD * c + f + 1)
                engine.tensor_tensor(y_lo[c % 2][:, f, :], v_fm[:, f, :], y_hi[c % 2][:, f, :].bitcast(f32), ALU.subtract).then_inc(y_lo_ok, 1)

        block = ctx.enter_context(nc.Block())

        @block.sync
        def _(sp):
            sp.dma_start(c_sb[:, :], c_d).then_inc(c_in, 16)
            tok_v = x_d.rearrange("a (c t p) d -> p (a c) t d", p=P, t=TT)
            sp.dma_start(wmod[:, :, D:2 * D], wmod_d[:, :, D:2 * D]).then_inc(wmod_in[0], 16)
            for t in range(0, TT, 2):
                sp.dma_start(tok[:, 0, t:t + 2], tok_v[:, 0, t:t + 2]).then_inc(tok_first_in[t // 2], 16)
            sp.dma_start(wmod[:, :, 0:D], wmod_d[:, :, 0:D]).then_inc(wmod_in[1], 16)
            sp.dma_start(wqkv_raw[:, :, :, :], wqkv_d).then_inc(wqkv_in, 16)
            sp.dma_start(wmod[:, :, 2 * D:3 * D], wmod_d[:, :, 2 * D:3 * D]).then_inc(wmod_in[2], 16)
            sp.dma_start(tok[:, 1], tok_v[:, 1]).then_inc(tok_in[1], 16)
            for js, done in ((slice(0, 2), w_first_in), (slice(2, J), w_in[MIX])):
                sp.dma_start(up_raw[MIX][:, js], wmix_up_d[:, js]).then_inc(done, 16)
                sp.dma_start(down_raw[MIX][:, js], wmix_out_d[:, js]).then_inc(done, 16)
                if js.start == 0:
                    sp.dma_start(wmod[:, :, 3 * D:6 * D], wmod_d[:, :, 3 * D:6 * D]).then_inc(wmod_in[3], 16)
            half = J // 2
            for n in range(2):
                sp.dma_start(up_raw[FFN][:, n * half:(n + 1) * half], wffn_up_d[:, n * half:(n + 1) * half]).then_inc(w_in[FFN], 16)
            sp.dma_start(down_raw[FFN][:, :, :], wffn_down_d).then_inc(w_in[FFN], 16)
            for c in range(2, NC):
                sp.dma_start(tok[:, c], tok_v[:, c]).then_inc(tok_in[c], 16)
            out_v = out_d.rearrange("a (c t p) d -> p (a c) t d", p=P, t=TT)
            for c in range(NC):
                for f in range(2):
                    sp.wait_ge(tr_free[f], turn("back", BLOCKS.index((FFN, c))) + 1)
                    sp.dma_start(out_v[:, c, 2 * f:2 * f + 2], tok[:, c, 2 * f:2 * f + 2]).then_inc(stored, 16)
            sp.wait_ge(stored, 16 * 2 * NC)

        @block.tensor
        def _(pe):
            def modulation(m, part, bank):
                pe.wait_ge(wmod_in[part], 16)
                for k in range(KD):
                    last = nc.tensor.matmul(bank[:, 0:D], silu_c_wide[:, k, :], wmod[:, k, m * D:(m + 1) * D], start=k == 0, stop=k == KD - 1)
                last.then_inc(mod_ps_ok, 1)

            def modulation_column(m):
                pe.wait_ge(wmod_in[2], 16)
                pe.wait_ge(wmod_in[3], 16)
                for f in range(KD):
                    for k in range(KD):
                        col = m * D + f * P
                        last = nc.tensor.matmul(up_ps[0][:, m * KD + f:m * KD + f + 1], wmod[:, k, col:col + P],
                                                silu_c[:, k:k + 1], start=k == 0, stop=k == KD - 1)
                last.then_inc(col_ps_ok, 1)

            def transit_transpose(what, which, src):
                n = turn(what, which)
                for f in range(KD):
                    if n >= 1:
                        pe.wait_ge(tr_free[f], n)
                    for t in range(TT):
                        last = nc.tensor.transpose(tr_ps[f][:, t * P:(t + 1) * P], src[:, t, f * P:(f + 1) * P], ident[:, :])
                    last.then_inc(tr_full[f], 1)

            def transit_h(c):
                pe.wait_ge(hs_ok, c + 2)
                transit_transpose("h", c, hs_tok)

            def transit_x(c):
                pe.wait_ge(x2_ok, c + 1)
                transit_transpose("x", c, x2_tok)

            def transit_back(b):
                n = turn("back", b)
                pe.wait_ge(out_taken, KD * (b + 1))
                for g in range(2):
                    pe.wait_ge(tr_free[g], n)
                    for u in range(2):
                        for f in range(KD):
                            col = (u * KD + f) * P
                            tt = 2 * g + u
                            last = nc.tensor.transpose(tr_ps[g][:, col:col + P], out_fm[:, f, tt * P:(tt + 1) * P], ident[:, :])
                    last.then_inc(tr_full[g], 1)

            def project(what, c, tiles=range(KD)):
                part = PARTS.index(what)
                if what == "k":
                    for f in range(KD):
                        pe.wait_ge(tr_free[f], turn("h", c) + 1)
                if c == 0:
                    pe.wait_ge(wqkv_lo_ok, part + 1)
                for f in tiles:
                    if early(what, c):
                        pe.wait_ge(early_free, f + 1)
                    else:
                        pe.wait_ge(tr_free[f], turn(what, c))
                    bank = out_ps[f] if early(what, c) else tr_ps[f]
                    cols_f = slice(f * P, (f + 1) * P)
                    for k in range(KD):
                        nc.tensor.matmul(bank[:, :], wqkv_hi[:, part, k, cols_f], h_hi[:, k, :], start=k == 0, stop=False)
                        nc.tensor.matmul(bank[:, :], wqkv_hi[:, part, k, cols_f], h_lo[:, k, :], start=False, stop=False)
                        last = nc.tensor.matmul(bank[:, :], wqkv_lo[:, part, k, cols_f], h_hi[:, k, :], start=False, stop=k == KD - 1)
                    last.then_inc(arrived(what, c, f)[0], 1)

            def sum_first_k():
                for f in range(KD):
                    pe.wait_ge(tr_free[f], turn("k", 0) + 1)
                    last = nc.tensor.matmul(out_ps[0][:, :], ones[:, :], sq_k0[:, f, :], start=f == 0, stop=f == KD - 1)
                last.then_inc(early_full, 1)

            def sum_first_q():
                pe.wait_ge(q_sum_ok, 1)
                nc.tensor.matmul(out_ps[1][:, :], ones[:, :], sq_q0[:, 0, :], start=True, stop=True).then_inc(early_full, 1)

            def sums(c):
                n = turn("s", c)
                for f in range(2):
                    pe.wait_ge(ss_ok, 2 * (c - 1) + f + 1)
                    pe.wait_ge(tr_free[f], n)
                    nc.tensor.matmul(tr_ps[f][:, :], ones_r[:, :], ss_hi[f][:, :], start=True, stop=False)
                    nc.tensor.matmul(tr_ps[f][:, :], ones_r[:, :], ss_lo[f][:, :], start=False, stop=True).then_inc(tr_full[f], 1)

            def hidden_tile(t):
                b, j = divmod(t, J)
                layer, c = BLOCKS[b]
                src_hi, src_lo = (y_hi[c % 2], y_lo[c % 2]) if layer == MIX else (x2_hi, x2_lo)
                if j == 0:
                    pe.wait_ge(y_lo_ok if layer == MIX else x2_lo_ok, KD * (c + 1))
                if c == 0:
                    pe.wait_ge(w_lo_ok[layer][j], 1)
                hi, lo = up_hi[layer], up_lo[layer]
                for which, bank, bank_read, full in ((1, gate_ps[t % 2], silu_ok, gate_full), (0, up_ps[t % 2], hid_ok, up_full)):
                    if t >= 2:
                        pe.wait_ge(bank_read, t - 1)
                    for k in range(KD):
                        nc.tensor.matmul(bank[:, :], hi[:, j, k, which, :], src_hi[:, k, :], start=k == 0, stop=False)
                        nc.tensor.matmul(bank[:, :], hi[:, j, k, which, :], src_lo[:, k, :], start=False, stop=False)
                        last = nc.tensor.matmul(bank[:, :], lo[:, j, k, which, :], src_hi[:, k, :], start=False, stop=k == KD - 1)
                    last.then_inc(full, 1)

            def down_tile(t):
                b, j = divmod(t, J)
                layer, c = BLOCKS[b]
                pe.wait_ge(hid_lo_ok, t + 1)
                if c == 0:
                    pe.wait_ge(w_lo_ok[layer][j], 2)
                if t == 0:
                    pe.wait_ge(early_free, 2 * KD)
                elif j == 0:
                    pe.wait_ge(out_taken, KD * b)
                hi, lo = down_hi[layer], down_lo[layer]
                s = t % HS_SLOTS
                for f in range(KD):
                    cols_f = slice(f * P, (f + 1) * P)
                    nc.tensor.matmul(out_ps[f][:, :], hi[:, j, cols_f], hid_hi[:, s, :], start=j == 0, stop=False)
                    nc.tensor.matmul(out_ps[f][:, :], hi[:, j, cols_f], hid_lo[:, s, :], start=False, stop=False)
                    last = nc.tensor.matmul(out_ps[f][:, :], lo[:, j, cols_f], hid_hi[:, s, :], start=False, stop=j == J - 1)
                    if t == NB * J - 1 and f == 0:
                        last.then_inc(last_half, 1)
                last.then_inc(down_done, 1)

            pe.wait_ge(wide_ok, KD)
            modulation(1, 0, gate_ps[1])
            modulation(0, 1, gate_ps[0])
            modulation(2, 2, up_ps[1])
            pe.wait_ge(ident_ok, 1)
            transit_h(0)
            project("k", 0)
            project("q", 0, [0])
            sum_first_k()
            project("q", 0, [1])
            project("v", 0, [0])
            modulation_column(2)
            sum_first_q()
            project("v", 0, [1])
            modulation_column(3)
            transit_h(1)
            modulation_column(4)
            modulation_column(5)
            project("k", 1)
            project("q", 1)
            pe.wait_ge(ones_ok, 1)
            pe.wait_ge(mod_ok, 1)
            pe.wait_ge(col_sb_ok, 1)
            for t in range(NB * J):
                b, j = divmod(t, J)
                hidden_tile(t)
                if t >= LAG:
                    down_tile(t - LAG)
                if b == 0:
                    if j == 1:
                        project("v", 1)
                    if j == 2:
                        sums(1)
                elif j == 0 and b - 1 in SCAN_IN and b > 1:
                    transit_x(BLOCKS[b - 2][1])
                elif b in PROJECT_IN:
                    c = PROJECT_IN[b]
                    if j == 2:
                        transit_back(b - 1)
                    if j == 4:
                        transit_h(c)
                    if j in (5, 6):
                        project("kq"[j - 5], c)
                    if j == 6 and BLOCKS[b - 1][0] == MIX:
                        transit_x(BLOCKS[b - 1][1])
                    if j == 7:
                        project("v", c)
                elif b in SCAN_IN:
                    if j == 1:
                        sums(SCAN_IN[b])
                    if j == 4:
                        transit_back(b - 1)
                else:
                    if j == 2:
                        transit_back(b - 1)
                    if j == 6 and BLOCKS[b - 1][0] == MIX:
                        transit_x(BLOCKS[b - 1][1])
            for t in range(NB * J - LAG, NB * J):
                down_tile(t)
            transit_back(NB - 1)

        @block.scalar
        def _(act):
            act_steps = [0]

            def take_h(c):
                n = turn("h", c)
                for f in range(KD):
                    act.wait_ge(tr_full[f], n + 1)
                    nc.scalar.activation(h_hi[:, f, :], tr_ps[f][:, :], ACT.Copy).then_inc(h_hi_ok, 1)

            def take_squares(what, c, tiles=range(KD)):
                dst, sq = q_fm if what == "q" else k_fm, squares(what, c)
                if c >= 1:
                    act.wait_ge(y_ok, KD * c)
                if c >= 1 and what == "k":
                    act.wait_ge(resid_ok, c + 1)
                for f in tiles:
                    bank = out_ps[f] if early(what, c) else tr_ps[f]
                    act.wait_ge(*arrived(what, c, f))
                    nc.scalar.activation(dst[:, f, :], bank[:, :], ACT.Copy)
                    nc.scalar.activation(sq[:, f, :], bank[:, :], ACT.Square).then_inc(taken(what, c, f)[0], 1)

            def take_v(c, tiles=range(KD)):
                n = turn("v", c)
                if c >= 1:
                    act.wait_ge(y_lo_ok, KD * c)
                for f in tiles:
                    act.wait_ge(tr_full[f], n + 1)
                    nc.scalar.activation(v_fm[:, f, :], tr_ps[f][:, :], ACT.Copy).then_inc(tr_free[f], 1)

            def rms_factor(c, f):
                r, done = ((squares("k", c)[:, 0, :], rk_ok), (squares("q", c)[:, 0, :], rq_ok))[f]
                if c == 0:
                    act.wait_ge(early_full, f + 1)
                    nc.scalar.activation(r, out_ps[f][:, :], ACT.Ln, scale=1.0 / D, bias=eps_col[:, :]).then_inc(early_free, 1)
                    act.wait_ge(early_free, f + 1)
                else:
                    n = turn("s", c)
                    act.wait_ge(tr_full[f], n + 1)
                    nc.scalar.activation(r, tr_ps[f][:, :], ACT.Ln, scale=1.0 / D, bias=eps_col[:, :]).then_inc(tr_free[f], 1)
                    act.wait_ge(tr_free[f], n + 1)
                nc.scalar.activation(r, r, ACT.Exp, scale=-0.5).then_inc(done, 1)

            def token_power(dst, src, by, plus, done):
                nc.scalar.activation(dst, src, ACT.Ln, scale=by, bias=plus).then_inc(act_step, 1)
                act_steps[0] += 1
                act.wait_ge(act_step, act_steps[0])
                nc.scalar.activation(dst, dst, ACT.Exp, scale=-0.5).then_inc(done, 1)

            def token_rstd(c):
                act.wait_ge(stats_ok, c + 1)
                token_power(rstd[:, :], mean_var[:, :, 1], 1.0, ln_eps_col[:, :], rstd_ok)

            def token_rms(c):
                act.wait_ge(h_sum_ok, c + 1)
                token_power(h_rms[:, :], h_sum[:, :], 1.0 / D, eps_col[:, :], h_rms_ok)

            def exp_k(c):
                for f in range(KD):
                    act.wait_ge(kn_ok[f], c + 1)
                    nc.scalar.activation(k_fm[:, f, :], k_fm[:, f, :], ACT.Exp).then_inc(w_ok, 1)

            def exp_q(c):
                for f in range(KD):
                    act.wait_ge(qn_ok[f], c + 1)
                    nc.scalar.activation(q_fm[:, f, :], q_fm[:, f, :], ACT.Exp, scale=-1.0).then_inc(e_ok, 1)

            def recip_guess(c):
                for f in range(KD):
                    act.wait_ge(den_ok, KD * c + f + 1)
                    nc.scalar.activation(k_fm[:, f, :], q_fm[:, f, :], ACT.Ln).then_inc(ln_ok, 1)
                    act.wait_ge(ln_ok, KD * c + f + 1)
                    nc.scalar.activation(k_fm[:, f, :], k_fm[:, f, :], ACT.Exp, scale=-1.0).then_inc(guess_ok, 1)

            def y_high(c):
                if c >= 2:
                    act.wait_ge(up_full, J * (BLOCKS.index((MIX, c - 2)) + 1))
                for f in range(KD):
                    act.wait_ge(y_ok, KD * c + f + 1)
                    nc.scalar.activation(y_hi[c % 2][:, f, :], v_fm[:, f, :], ACT.Copy).then_inc(y_hi_ok, 1)

            def h_squares(c):
                if c >= 2:
                    for f in range(KD):
                        act.wait_ge(qn_ok[f], c)
                for t in range(TT):
                    act.wait_ge(h_ok, h_ok_at(c, t))
                    last = nc.scalar.activation(hs_tok[:, t, :], h_tok[:, t, :], ACT.Square, accum_out=h_sum[:, t:t + 1])
                last.then_inc(h_sum_ok, 1)

            def take_out(b):
                layer, c = BLOCKS[b]
                if b >= 1:
                    act.wait_ge(tr_full[1], turn("back", b - 1) + 1)
                    if BLOCKS[b - 1][0] == MIX:
                        act.wait_ge(x2_lo_ok, KD * (BLOCKS[b - 1][1] + 1))
                else:
                    act.wait_ge(cols_ok, 1)
                act.wait_ge(down_done, J * (b + 1))
                gate = cols[:, 2 if layer == MIX else 5, :]
                for f in range(KD):
                    nc.scalar.activation(out_fm[:, f, :], out_ps[f][:, :], ACT.Copy, scale=gate[:, f:f + 1]).then_inc(out_taken, 1)

            def take_x(c):
                n = turn("x", c)
                for f in range(KD):
                    act.wait_ge(tr_full[f], n + 1)
                    nc.scalar.activation(x2_fm[:, f, :], tr_ps[f][:, :], ACT.Identity, scale=cols[:, 4, f:f + 1],
                                         bias=cols[:, 3, f:f + 1]).then_inc(tr_free[f], 1)
                if c >= 1:
                    act.wait_ge(up_full, J * (BLOCKS.index((FFN, c - 1)) + 1))
                for f in range(KD):
                    act.wait_ge(tr_free[f], n + 1)
                    nc.scalar.activation(x2_hi[:, f, :], x2_fm[:, f, :], ACT.Copy).then_inc(x2_hi_ok, 1)

            def split_hi(layer, j):
                nc.scalar.activation(up_hi[layer][:, j], up_raw[layer][:, j], ACT.Copy).then_inc(w_hi_ok[layer], 1)
                nc.scalar.activation(down_hi[layer][:, j], down_raw[layer][:, j], ACT.Copy).then_inc(w_hi_ok[layer], 1)

            def silu_tile(t):
                act.wait_ge(gate_full, t + 1)
                if t >= 2:
                    act.wait_ge(hid_lo_ok, t - 1)
                nc.scalar.activation(hid[:, t % 2, :], gate_ps[t % 2][:, :], ACT.Silu).then_inc(silu_ok, 1)

            def hi_tile(t):
                act.wait_ge(hid_ok, t + 1)
                if t >= HS_SLOTS:
                    act.wait_ge(down_done, t - HS_SLOTS + 1)
                nc.scalar.activation(hid_hi[:, t % HS_SLOTS, :], hid[:, t % 2, :], ACT.Copy).then_inc(hid_hi_ok, 1)

            act.wait_ge(c_in, 16)
            nc.scalar.activation(silu_c[:, :], c_sb[:, :], ACT.Silu).then_inc(silu_c_ok, 1)
            nc.scalar.preload_act_table_set(LN_EXP)
            act.wait_ge(consts, 1)
            token_rstd(0)
            h_squares(0)
            token_rms(0)
            act.wait_ge(h_rms_ok, 1)
            for t in range(TT // 2, TT):
                last = nc.scalar.activation(hs_tok[:, t, :], h_tok[:, t, :], ACT.Copy, scale=h_rms[:, t:t + 1])
            last.then_inc(hs_ok, 1)
            act.wait_ge(wqkv_in, 16)
            for part in range(3):
                nc.scalar.activation(wqkv_hi[:, part], wqkv_raw[:, part], ACT.Copy).then_inc(wqkv_hi_ok, 1)
            take_h(0)
            act.wait_ge(w_first_in, 32)
            for j in range(2):
                split_hi(MIX, j)
            take_squares("k", 0)
            token_rstd(1)
            take_squares("q", 0, [0])
            rms_factor(0, 0)
            take_squares("q", 0, [1])
            h_squares(1)
            token_rms(1)
            take_v(0, [0])
            exp_k(0)
            rms_factor(0, 1)
            take_v(0, [1])
            exp_q(0)
            take_h(1)
            recip_guess(0)
            act.wait_ge(col_ps_ok, 4)
            nc.scalar.activation(col_sb[:, 2 * KD:], up_ps[0][:, 2 * KD:6 * KD], ACT.Copy).then_inc(col_sb_ok, 1)
            y_high(0)
            nc.scalar.preload_act_table_set(SILU)
            act.wait_ge(w_in[MIX], 32)
            for j in (2, 3):
                split_hi(MIX, j)
            for t in range(NB * J + 1):
                b, j = divmod(t, J)
                if t >= 1 and not split_early(t - 1):
                    hi_tile(t - 1)
                if t < NB * J:
                    silu_tile(t)
                if b == NB:
                    break
                if b == 0:
                    if j == 0:
                        take_squares("k", 1)
                    if j == 1:
                        take_squares("q", 1)
                    if j < 4:
                        split_hi(MIX, j + 4)
                    if j == 2:
                        take_v(1)
                if b in SCAN_IN:
                    if j == SCAN_AT[b]:
                        nc.scalar.preload_act_table_set(LN_EXP)
                        rms_factor(SCAN_IN[b], 0)
                        rms_factor(SCAN_IN[b], 1)
                        hi_tile(t)
                    if j == SCAN_AT[b]:
                        exp_k(SCAN_IN[b])
                        exp_q(SCAN_IN[b])
                    if j == SCAN_AT[b] + 1:
                        hi_tile(t)
                    if j == SCAN_AT[b] + 2:
                        nc.scalar.preload_act_table_set(LN_EXP)
                        recip_guess(SCAN_IN[b])
                        hi_tile(t)
                    if j in (SCAN_AT[b], SCAN_AT[b] + 2):
                        nc.scalar.preload_act_table_set(SILU)
                    if j == SCAN_AT[b] + 3:
                        y_high(SCAN_IN[b])
                if b == 0:
                    continue
                if j == 1 and b - 1 in SCAN_IN and b >= 2:
                    take_x(BLOCKS[b - 2][1])
                if j == 1:
                    take_out(b - 1)
                if b == 1:
                    if j == 0:
                        act.wait_ge(w_in[FFN], 48)
                    split_hi(FFN, j)
                if b in PROJECT_IN:
                    c = PROJECT_IN[b]
                    if j == 2:
                        h_squares(c)
                    if j == 4:
                        take_h(c)
                    if j in (5, 6):
                        take_squares("kq"[j - 5], c)
                    if j == 7:
                        take_v(c)
                if b not in SCAN_IN and j == 6 and BLOCKS[b - 1][0] == MIX:
                    take_x(BLOCKS[b - 1][1])
            act.wait_ge(tr_full[1], turn("back", NB - 2) + 1)
            act.wait_ge(x2_lo_ok, KD * NC)
            act.wait_ge(last_half, 1)
            nc.scalar.activation(out_fm[:, 0, :], out_ps[0][:, :], ACT.Copy, scale=cols[:, 5, 0:1]).then_inc(out_taken, 1)

        @block.vector
        def _(dve):
            steps = [0]

            def link(ins):
                steps[0] += 1
                ins.then_inc(dve_step, 1)
                dve.wait_ge(dve_step, steps[0])

            def later(ins):
                steps[0] += 1
                ins.then_inc(dve_step, 1)

            def settle():
                dve.wait_ge(dve_step, steps[0])

            def modulated_norm(c):
                for t in range(TT):
                    later(nc.vector.scalar_tensor_tensor(out=h_tok[:, t, :], in0=tok[:, c, t, :], scalar=mean_var[:, t, 0:1],
                                                         in1=mod_scale[:, :], op0=ALU.subtract, op1=ALU.mult))
                if c == 0:
                    dve.wait_ge(mod_ps_ok, 2)
                    later(nc.vector.tensor_copy(mod_shift[:, :], gate_ps[0][:, 0:D]))
                settle()
                dve.wait_ge(rstd_ok, c + 1)
                for t in range(TT):
                    nc.vector.scalar_tensor_tensor(out=h_tok[:, t, :], in0=h_tok[:, t, :], scalar=rstd[:, t:t + 1],
                                                   in1=mod_shift[:, :], op0=ALU.mult, op1=ALU.add).then_inc(h_ok, 1)

            def token_stats(src, st, mv, done):
                for t in range(TT):
                    last = nc.vector.bn_stats(st[:, t, :], src[:, t, :])
                link(last)
                for t in range(TT):
                    last = nc.vector.bn_aggr(mv[:, t, :], st[:, t, :])
                last.then_inc(done, 1)

            def normalise(dst, src, mv, rs, rs_ok, n, done):
                dve.wait_ge(rs_ok, n)
                for t in range(TT):
                    last = nc.vector.tensor_scalar(dst[:, t, :], src[:, t, :], mv[:, t, 0:1], rs[:, t:t + 1], ALU.subtract, ALU.mult)
                last.then_inc(done, 1)

            def ln1_stats(c):
                dve.wait_ge(tok_in[c], 16)
                token_stats(tok[:, c], stats, mean_var, stats_ok)

            def ln1_normalise(c):
                dve.wait_ge(resid_ok, c)
                if c >= 2:
                    for f in range(KD):
                        dve.wait_ge(kn_ok[f], c)
                normalise(h_tok, tok[:, c], mean_var, rstd, rstd_ok, c + 1, norm_ok)

            def take_h(c):
                for f in range(KD):
                    dve.wait_ge(h_hi_ok, KD * c + f + 1)
                    nc.vector.tensor_tensor(h_lo[:, f, :], tr_ps[f][:, :], h_hi[:, f, :].bitcast(f32), ALU.subtract).then_inc(tr_free[f], 1)

            def scan(c, f):
                dve.wait_ge(w_ok, KD * c + f + 1)
                dve.wait_ge(tr_free[f], turn("v", c) + 1)
                link(nc.vector.scalar_tensor_tensor(out=v_fm[:, f, :], in0=v_fm[:, f, :], scalar=-1.0, in1=k_fm[:, f, :],
                                                    op0=ALU.mult, op1=ALU.mult))
                link(nc.vector.tensor_tensor_scan(k_fm[:, f, :], one_col[:, :].to_broadcast([P, CH]), k_fm[:, f, :],
                                                  carry[:, 0, f:f + 1], ALU.mult, ALU.add))
                link(nc.vector.tensor_tensor_scan(v_fm[:, f, :], one_col[:, :].to_broadcast([P, CH]), v_fm[:, f, :],
                                                  carry[:, 1, f:f + 1], ALU.mult, ALU.add))
                later(nc.vector.tensor_copy(carry[:, 0, f:f + 1], k_fm[:, f, CH - 1:CH]))
                later(nc.vector.tensor_copy(carry[:, 1, f:f + 1], v_fm[:, f, CH - 1:CH]))

            def denominator(c, f):
                dve.wait_ge(e_ok, KD * c + f + 1)
                nc.vector.scalar_tensor_tensor(out=q_fm[:, f, :], in0=q_fm[:, f, :], scalar=1.0, in1=k_fm[:, f, :],
                                               op0=ALU.add, op1=ALU.mult).then_inc(den_ok, 1)

            def newton_factor(c, f):
                dve.wait_ge(guess_ok, KD * c + f + 1)
                later(nc.vector.tensor_tensor(q_fm[:, f, :], q_fm[:, f, :], k_fm[:, f, :], ALU.mult))

            def quotient(c, f):
                dve.wait_ge(ng_ok, KD * c + f + 1)
                settle()
                nc.vector.scalar_tensor_tensor(out=v_fm[:, f, :], in0=q_fm[:, f, :], scalar=-2.0, in1=v_fm[:, f, :],
                                               op0=ALU.add, op1=ALU.mult).then_inc(y_ok, 1)

            def take_back(b):
                layer, c = BLOCKS[b]
                n = turn("back", b)
                if layer == MIX:
                    dve.wait_ge(resid_ok, c + 1)
                for g in range(2):
                    dve.wait_ge(tr_full[g], n + 1)
                    rows = tok[:, c, 2 * g:2 * g + 2, :].rearrange("p t d -> p (t d)")
                    nc.vector.tensor_tensor(rows, tr_ps[g][:, :], rows, ALU.add).then_inc(tr_free[g], 1)
                if layer == FFN:
                    return
                for g in range(2):
                    dve.wait_ge(tr_free[g], n + 1)
                token_stats(tok[:, c], stats2, mean_var2, stats2_ok)

            def normalise_x(c):
                if c >= 1:
                    for f in range(KD):
                        dve.wait_ge(tr_full[f], turn("x", c - 1) + 1)
                normalise(x2_tok, tok[:, c], mean_var2, rstd2, rstd2_ok, c + 1, x2_ok)

            def take_x(c):
                for f in range(KD):
                    dve.wait_ge(x2_hi_ok, KD * c + f + 1)
                    nc.vector.tensor_tensor(x2_lo[:, f, :], x2_fm[:, f, :], x2_hi[:, f, :].bitcast(f32), ALU.subtract).then_inc(x2_lo_ok, 1)

            def mul_tile(t):
                dve.wait_ge(silu_ok, t + 1)
                dve.wait_ge(up_full, t + 1)
                nc.vector.tensor_tensor(hid[:, t % 2, :], up_ps[t % 2][:, :], hid[:, t % 2, :], ALU.mult).then_inc(hid_ok, 1)

            def lo_tile(t):
                dve.wait_ge(hid_hi_ok, t + 1)
                s = t % HS_SLOTS
                nc.vector.tensor_tensor(hid_lo[:, s, :], hid[:, t % 2, :], hid_hi[:, s, :].bitcast(f32), ALU.subtract).then_inc(hid_lo_ok, 1)

            nc.vector.memset(one_col[:, :], 1.0)
            nc.vector.memset(eps_col[:, :], RMS_EPS)
            nc.vector.memset(ln_eps_col[:, :], LN_EPS)
            nc.vector.memset(carry[:, 0, :], CUM_EPS)
            nc.vector.memset(carry[:, 1, :], 0.0)
            nc.vector.memset(ones_r[:, :].bitcast(f32), 1.0).then_inc(ones_ok, 1)
            link(nc.vector.memset(ones[:, :], 1.0))
            nc.vector.memset(minus_half[:, :], -0.5).then_inc(consts, 1)
            dve.wait_ge(silu_c_ok, 1)
            for k in range(KD):
                nc.vector.tensor_scalar(silu_c_wide[:, k, :], ones[:, :], silu_c[:, k:k + 1], None, ALU.mult).then_inc(wide_ok, 1)
            for t in range(TT):
                if t % 2 == 0:
                    dve.wait_ge(tok_first_in[t // 2], 16)
                later(nc.vector.bn_stats(stats[:, t, :], tok[:, 0, t, :]))
            settle()
            for t in range(TT):
                last = nc.vector.bn_aggr(mean_var[:, t, :], stats[:, t, :])
            last.then_inc(stats_ok, 1)
            dve.wait_ge(mod_ps_ok, 1)
            later(nc.vector.tensor_scalar(mod_scale[:, :], gate_ps[1][:, 0:D], 1.0, None, ALU.add))
            settle()
            dve.wait_ge(stats_ok, 1)
            modulated_norm(0)
            dve.wait_ge(h_rms_ok, 1)
            for t in range(TT // 2):
                last = nc.vector.tensor_scalar(hs_tok[:, t, :], h_tok[:, t, :], h_rms[:, t:t + 1], None, ALU.mult)
            last.then_inc(hs_ok, 1)
            take_h(0)
            def gate_of(dst, src, tmp):
                link(nc.vector.tensor_scalar(tmp, src, 0.0, 2.0, ALU.is_ge, ALU.mult))
                link(nc.vector.tensor_scalar(dst, src, GATE_MIN, None, ALU.max))
                link(nc.vector.scalar_tensor_tensor(out=dst, in0=src, scalar=-1.0, in1=dst, op0=ALU.mult, op1=ALU.max))
                return nc.vector.scalar_tensor_tensor(out=dst, in0=tmp, scalar=-1.0, in1=dst, op0=ALU.add, op1=ALU.mult)

            dve.wait_ge(mod_ps_ok, 3)
            gate_of(gate_tok[:, :], up_ps[1][:, 0:D], out_fm[:, 0, 0:D]).then_inc(mod_ok, 1)
            dve.wait_ge(hs_ok, 2)
            dve.wait_ge(mod_ok, 1)
            nc.vector.tensor_tensor(h_tok[:, :, :], h_tok[:, :, :], gate_tok[:, :].unsqueeze(1).to_broadcast([P, TT, D]),
                                    ALU.mult).then_inc(gated_ok, 1)
            ln1_stats(1)
            dve.wait_ge(resid_ok, 1)
            dve.wait_ge(stats_ok, 2)
            modulated_norm(1)
            for f in range(KD):
                dve.wait_ge(tr_free[f], turn("q", 0) + 1)
            nc.vector.tensor_tensor(sq_q0[:, 0, :], sq_q0[:, 0, :], sq_q0[:, 1, :], ALU.add).then_inc(q_sum_ok, 1)
            norm(nc.vector, dve.wait_ge, "k", 0, 0)
            scan(0, 0)
            norm(nc.vector, dve.wait_ge, "q", 0, 1)
            scan(0, 1)
            take_h(1)
            denominator(0, 0)
            denominator(0, 1)
            for f in range(KD):
                newton_factor(0, f)
                quotient(0, f)
            y_low(nc.vector, dve.wait_ge, 0)
            dve.wait_ge(col_sb_ok, 1)
            col_m = col_sb[:, :].rearrange("p (m f) -> p m f", f=KD)
            link(gate_of(cols[:, 2, :], col_m[:, 2, :], col_t[:, 0, :]))
            link(gate_of(cols[:, 5, :], col_m[:, 5, :], col_t[:, 1, :]))
            nc.vector.tensor_copy(cols[:, 3, :], col_m[:, 3, :])
            nc.vector.tensor_scalar(cols[:, 4, :], col_m[:, 4, :], 1.0, None, ALU.add).then_inc(cols_ok, 1)
            for t in range(NB * J + 1):
                b, j = divmod(t, J)
                if t >= 1 and not split_early(t - 1):
                    lo_tile(t - 1)
                if t < NB * J:
                    mul_tile(t)
                if b == NB:
                    break
                if b in SCAN_IN:
                    c = SCAN_IN[b]
                    if b == 0 and j == 1:
                        sums_of_squares(nc.vector, dve.wait_ge, link, c)
                    if j == SCAN_AT[b]:
                        norm(nc.vector, dve.wait_ge, "k", c, 0)
                        norm(nc.vector, dve.wait_ge, "q", c, 1)
                        lo_tile(t)
                    for f in range(KD):
                        if j == SCAN_AT[b] + f:
                            scan(c, f)
                            if f == 1:
                                lo_tile(t)
                            denominator(c, f)
                        if j == SCAN_AT[b] + 2:
                            if f == 1:
                                lo_tile(t)
                            newton_factor(c, f)
                            quotient(c, f)
                if j == J - 1 and b + 1 in PROJECT_IN:
                    ln1_stats(PROJECT_IN[b + 1])
                if b == 0:
                    continue
                if j == 1 and b - 1 in SCAN_IN and b >= 2:
                    take_x(BLOCKS[b - 2][1])
                if b in PROJECT_IN:
                    if j == 0:
                        ln1_normalise(PROJECT_IN[b])
                    if j == 4:
                        take_h(PROJECT_IN[b])
                back_at = 5 if b in SCAN_IN else 2
                if j == back_at:
                    take_back(b - 1)
                if j == back_at + 1 and BLOCKS[b - 1][0] == MIX:
                    normalise_x(BLOCKS[b - 1][1])
                if b not in SCAN_IN and j == 6 and BLOCKS[b - 1][0] == MIX:
                    take_x(BLOCKS[b - 1][1])
            dve.wait_ge(down_done, J * NB)
            nc.vector.tensor_scalar(out_fm[:, 1, :], out_ps[1][:, :], cols[:, 5, 1:2], None, ALU.mult).then_inc(out_taken, 1)
            take_back(NB - 1)

        @block.gpsimd
        def _(pool):
            steps = [0]

            def link(ins):
                steps[0] += 1
                ins.then_inc(pool_step, 1)
                pool.wait_ge(pool_step, steps[0])

            def power_of(dst, src, by, plus, done):
                link(nc.gpsimd.tensor_scalar(dst, src, by, plus, ALU.mult, ALU.add))
                nc.gpsimd.tensor_tensor(dst, dst, minus_half[:, :], ALU.pow).then_inc(done, 1)

            def token_rstd(c):
                pool.wait_ge(stats_ok, c + 1)
                power_of(rstd[:, :], mean_var[:, :, 1], 1.0, LN_EPS, rstd_ok)

            def token_rstd2(c):
                pool.wait_ge(stats2_ok, c + 1)
                power_of(rstd2[:, :], mean_var2[:, :, 1], 1.0, LN_EPS, rstd2_ok)

            def token_rms(c):
                pool.wait_ge(h_sum_ok, c + 1)
                power_of(h_rms[:, :], h_sum[:, :], 1.0 / D, RMS_EPS, h_rms_ok)

            def modulate(c):
                pool.wait_ge(norm_ok, c - 1)
                wide = mod_scale[:, :].unsqueeze(1).to_broadcast([P, TT, D])
                link(nc.gpsimd.tensor_tensor(h_tok[:, :, :], h_tok[:, :, :], wide, ALU.mult))
                wide = mod_shift[:, :].unsqueeze(1).to_broadcast([P, TT, D])
                nc.gpsimd.tensor_tensor(h_tok[:, :, :], h_tok[:, :, :], wide, ALU.add).then_inc(h_ok, 1)

            def scale_by_rms(c):
                pool.wait_ge(h_rms_ok, c + 1)
                for t in range(TT):
                    last = nc.gpsimd.tensor_scalar(hs_tok[:, t, :], h_tok[:, t, :], h_rms[:, t:t + 1], 0.0, ALU.mult, ALU.add)
                last.then_inc(hs_ok, 1)

            def residual(c):
                pool.wait_ge(mod_ok, 1)
                pool.wait_ge(hs_ok, c + 2)
                wide = gate_tok[:, :].unsqueeze(1).to_broadcast([P, TT, D])
                link(nc.gpsimd.tensor_tensor(h_tok[:, :, :], h_tok[:, :, :], wide, ALU.mult))
                nc.gpsimd.tensor_tensor(tok[:, c], tok[:, c], h_tok[:, :, :], ALU.add).then_inc(resid_ok, 1)

            def guess_times_num(c):
                for f in range(KD):
                    pool.wait_ge(guess_ok, KD * c + f + 1)
                    nc.gpsimd.tensor_tensor(v_fm[:, f, :], v_fm[:, f, :], k_fm[:, f, :], ALU.mult).then_inc(ng_ok, 1)

            link(nc.gpsimd.memset(ident[:, :], 0.0))
            nc.gpsimd.affine_select(out=ident[:, :], in_=ident[:, :], compare_op=ALU.not_equal, fill=1.0, base=0,
                                    pattern=[[-1, P]], channel_multiplier=1).then_inc(ident_ok, 1)
            pool.wait_ge(consts, 1)
            for part in range(3):
                pool.wait_ge(wqkv_hi_ok, part + 1)
                nc.gpsimd.tensor_tensor(wqkv_lo[:, part], wqkv_raw[:, part], wqkv_hi[:, part].bitcast(f32), ALU.subtract).then_inc(wqkv_lo_ok, 1)
            pool.wait_ge(gated_ok, 1)
            nc.gpsimd.tensor_tensor(tok[:, 0], tok[:, 0], h_tok[:, :, :], ALU.add).then_inc(resid_ok, 1)
            for j in range(2):
                split_lo(nc.gpsimd, pool.wait_ge, MIX, j)
            norm(nc.gpsimd, pool.wait_ge, "k", 0, 1)
            scale_by_rms(1)
            norm(nc.gpsimd, pool.wait_ge, "q", 0, 0)
            residual(1)
            guess_times_num(0)
            for j in range(2, 6):
                split_lo(nc.gpsimd, pool.wait_ge, MIX, j)
            for b in range(NB):
                if b in PROJECT_IN:
                    c = PROJECT_IN[b]
                    token_rstd(c)
                    modulate(c)
                    if BLOCKS[b - 1][0] == MIX:
                        token_rstd2(BLOCKS[b - 1][1])
                    token_rms(c)
                    scale_by_rms(c)
                    residual(c)
                    if b == 1:
                        for j in range(4):
                            split_lo(nc.gpsimd, pool.wait_ge, FFN, j)
                    sums_of_squares(nc.gpsimd, pool.wait_ge, link, c)
                    if b == 1:
                        for j in range(4, J):
                            split_lo(nc.gpsimd, pool.wait_ge, FFN, j)
                elif b in SCAN_IN:
                    norm(nc.gpsimd, pool.wait_ge, "k", SCAN_IN[b], 1)
                    norm(nc.gpsimd, pool.wait_ge, "q", SCAN_IN[b], 0)
                    if b == 0:
                        for j in range(6, J):
                            split_lo(nc.gpsimd, pool.wait_ge, MIX, j)
                    guess_times_num(SCAN_IN[b])
                    y_low(nc.gpsimd, pool.wait_ge, SCAN_IN[b])
                if b not in PROJECT_IN and b >= 1 and BLOCKS[b - 1][0] == MIX:
                    token_rstd2(BLOCKS[b - 1][1])


def kernel(L0_attn_x, L0_attn_w_qkv, L0_attn_w_swiglu, L0_attn_w_out, L0_ffn_w_gate, L0_ffn_w_up, L0_ffn_w_down, L0_c, L0_wmod):
    import numpy as np
    import concourse.bacc as bacc
    from concourse.bass_utils import run_bass_kernel_spmd

    def lay(a, shape, order):
        return np.ascontiguousarray(np.asarray(a).reshape(shape).transpose(order))

    arrays = {
        "x": np.ascontiguousarray(L0_attn_x),
        "c": lay(L0_c, (KD, P), (1, 0)),
        "wmod": lay(L0_wmod, (KD, P, 6 * D), (1, 0, 2)),
        "wqkv": lay(np.asarray(L0_attn_w_qkv).reshape(3, D, D)[[1, 0, 2]], (3, D, KD, P), (3, 0, 2, 1)),
        "wmix_up": lay(L0_attn_w_swiglu, (2, J, P, KD, P), (4, 1, 3, 0, 2)),
        "wmix_out": lay(L0_attn_w_out, (D, J, P), (2, 1, 0)),
        "wffn_up": lay(np.stack([np.asarray(L0_ffn_w_up), np.asarray(L0_ffn_w_gate)]), (2, J, P, KD, P), (4, 1, 3, 0, 2)),
        "wffn_down": lay(L0_ffn_w_down, (D, J, P), (2, 1, 0)),
    }
    nc = bacc.Bacc("TRN2", target_bir_lowering=False, num_devices=1)
    f32 = mybir.dt.float32
    ins = [nc.dram_tensor(n, a.shape, f32, kind="ExternalInput").ap() for n, a in arrays.items()]
    out = nc.dram_tensor("out", (1, S, D), f32, kind="ExternalOutput").ap()
    adaln_kernel(nc, *ins, out)
    return run_bass_kernel_spmd(nc, [arrays], core_ids=[0]).results[0]["out"]
```
